# Optimizing a Trainium2 kernel written in Bass

```python
import numpy as np
import jax
import jax.numpy as jnp

def _softmax(x, axis=-1):
    return jax.nn.softmax(x, axis=axis)

def _gelu(x):
    return jax.nn.gelu(x, approximate=True)

def _silu(x):
    return jax.nn.silu(x)

def _sigmoid(x):
    return jax.nn.sigmoid(x)

def _layernorm(x, axis=-1, eps=1e-05):
    m = jnp.mean(x, axis=axis, keepdims=True)
    v = jnp.var(x, axis=axis, keepdims=True)
    return (x - m) / jnp.sqrt(v + eps)

def _scatter_add(tgt, idx, src, axis=0):
    return tgt.at[idx].add(src)

def _segment_sum(src, seg, n):
    return jax.ops.segment_sum(src, seg, n)
kernel_name = 'mk_dlrm_tower_d1_rec_r8_5b49fd'

def setup_inputs(seed: int=0):
    np.random.seed(seed)
    _w = jnp.asarray

    def _rec_inputs():
        import jax
        import jax.numpy as jnp
        _tk = jax.random.key(seed)
        dense_ctx = jax.random.normal(jax.random.fold_in(_tk, 190), (512, 16), jnp.float32)
        ids = jnp.stack([jax.random.randint(jax.random.fold_in(_tk, 200 + f), (512,), 0, v, jnp.int32) for f, v in enumerate([12500, 125000, 1000, 12500, 125000, 1250, 12500, 1250, 12500, 125000, 1250, 1000, 1000, 1000, 12500, 1000, 1250, 1250, 12500, 1250, 12500, 1000, 1250, 1250, 12500, 1000, 1000, 1000, 1250, 1000, 1000, 1000])], axis=1)
        tbl_0 = 0.05 * jax.random.normal(jax.random.fold_in(_tk, 500 + 0), (12500, 64), jnp.float32)
        tbl_1 = 0.05 * jax.random.normal(jax.random.fold_in(_tk, 500 + 1), (125000, 64), jnp.float32)
        tbl_2 = 0.05 * jax.random.normal(jax.random.fold_in(_tk, 500 + 2), (1000, 64), jnp.float32)
        tbl_3 = 0.05 * jax.random.normal(jax.random.fold_in(_tk, 500 + 3), (12500, 64), jnp.float32)
        tbl_4 = 0.05 * jax.random.normal(jax.random.fold_in(_tk, 500 + 4), (125000, 64), jnp.float32)
        tbl_5 = 0.05 * jax.random.normal(jax.random.fold_in(_tk, 500 + 5), (1250, 64), jnp.float32)
        tbl_6 = 0.05 * jax.random.normal(jax.random.fold_in(_tk, 500 + 6), (12500, 64), jnp.float32)
        tbl_7 = 0.05 * jax.random.normal(jax.random.fold_in(_tk, 500 + 7), (1250, 64), jnp.float32)
        tbl_8 = 0.05 * jax.random.normal(jax.random.fold_in(_tk, 500 + 8), (12500, 64), jnp.float32)
        tbl_9 = 0.05 * jax.random.normal(jax.random.fold_in(_tk, 500 + 9), (125000, 64), jnp.float32)
        tbl_10 = 0.05 * jax.random.normal(jax.random.fold_in(_tk, 500 + 10), (1250, 64), jnp.float32)
        tbl_11 = 0.05 * jax.random.normal(jax.random.fold_in(_tk, 500 + 11), (1000, 64), jnp.float32)
        tbl_12 = 0.05 * jax.random.normal(jax.random.fold_in(_tk, 500 + 12), (1000, 64), jnp.float32)
        tbl_13 = 0.05 * jax.random.normal(jax.random.fold_in(_tk, 500 + 13), (1000, 64), jnp.float32)
        tbl_14 = 0.05 * jax.random.normal(jax.random.fold_in(_tk, 500 + 14), (12500, 64), jnp.float32)
        tbl_15 = 0.05 * jax.random.normal(jax.random.fold_in(_tk, 500 + 15), (1000, 64), jnp.float32)
        tbl_16 = 0.05 * jax.random.normal(jax.random.fold_in(_tk, 500 + 16), (1250, 64), jnp.float32)
        tbl_17 = 0.05 * jax.random.normal(jax.random.fold_in(_tk, 500 + 17), (1250, 64), jnp.float32)
        tbl_18 = 0.05 * jax.random.normal(jax.random.fold_in(_tk, 500 + 18), (12500, 64), jnp.float32)
        tbl_19 = 0.05 * jax.random.normal(jax.random.fold_in(_tk, 500 + 19), (1250, 64), jnp.float32)
        tbl_20 = 0.05 * jax.random.normal(jax.random.fold_in(_tk, 500 + 20), (12500, 64), jnp.float32)
        tbl_21 = 0.05 * jax.random.normal(jax.random.fold_in(_tk, 500 + 21), (1000, 64), jnp.float32)
        tbl_22 = 0.05 * jax.random.normal(jax.random.fold_in(_tk, 500 + 22), (1250, 64), jnp.float32)
        tbl_23 = 0.05 * jax.random.normal(jax.random.fold_in(_tk, 500 + 23), (1250, 64), jnp.float32)
        tbl_24 = 0.05 * jax.random.normal(jax.random.fold_in(_tk, 500 + 24), (12500, 64), jnp.float32)
        tbl_25 = 0.05 * jax.random.normal(jax.random.fold_in(_tk, 500 + 25), (1000, 64), jnp.float32)
        tbl_26 = 0.05 * jax.random.normal(jax.random.fold_in(_tk, 500 + 26), (1000, 64), jnp.float32)
        tbl_27 = 0.05 * jax.random.normal(jax.random.fold_in(_tk, 500 + 27), (1000, 64), jnp.float32)
        tbl_28 = 0.05 * jax.random.normal(jax.random.fold_in(_tk, 500 + 28), (1250, 64), jnp.float32)
        tbl_29 = 0.05 * jax.random.normal(jax.random.fold_in(_tk, 500 + 29), (1000, 64), jnp.float32)
        tbl_30 = 0.05 * jax.random.normal(jax.random.fold_in(_tk, 500 + 30), (1000, 64), jnp.float32)
        tbl_31 = 0.05 * jax.random.normal(jax.random.fold_in(_tk, 500 + 31), (1000, 64), jnp.float32)
        _rk = jax.random.fold_in(_tk, 7)
        W_top1 = 0.0606339 * jax.random.normal(jax.random.fold_in(_tk, 801), (272, 512), jnp.float32)
        W_top2 = 0.0441942 * jax.random.normal(jax.random.fold_in(_tk, 802), (512, 256), jnp.float32)
        W_top3 = 0.0625 * jax.random.normal(jax.random.fold_in(_tk, 803), (256, 1), jnp.float32)
        b_top1 = jnp.zeros((512,), jnp.float32)
        b_top2 = jnp.zeros((256,), jnp.float32)
        return (dense_ctx, ids, tbl_0, tbl_1, tbl_2, tbl_3, tbl_4, tbl_5, tbl_6, tbl_7, tbl_8, tbl_9, tbl_10, tbl_11, tbl_12, tbl_13, tbl_14, tbl_15, tbl_16, tbl_17, tbl_18, tbl_19, tbl_20, tbl_21, tbl_22, tbl_23, tbl_24, tbl_25, tbl_26, tbl_27, tbl_28, tbl_29, tbl_30, tbl_31, W_top1, b_top1, W_top2, b_top2, W_top3)
    dense_ctx, ids, tbl_0, tbl_1, tbl_2, tbl_3, tbl_4, tbl_5, tbl_6, tbl_7, tbl_8, tbl_9, tbl_10, tbl_11, tbl_12, tbl_13, tbl_14, tbl_15, tbl_16, tbl_17, tbl_18, tbl_19, tbl_20, tbl_21, tbl_22, tbl_23, tbl_24, tbl_25, tbl_26, tbl_27, tbl_28, tbl_29, tbl_30, tbl_31, W_top1, b_top1, W_top2, b_top2, W_top3 = _rec_inputs()

    def _L0_rec_setup():
        import jax, jax.numpy as jnp
        import numpy as np
        B, NF, EMB = (256, 32, 64)
        FEAT_MAP_DIM = [128, 128, 128]
        key = jax.random.key(seed)
        ks = jax.random.split(key, 7)
        inp = jax.random.normal(ks[0], (B, NF, EMB), dtype=jnp.float32)
        in_chs = [NF * NF, FEAT_MAP_DIM[0] // 2 * NF, FEAT_MAP_DIM[1] // 2 * NF]
        params = {}
        for i, (ic, oc) in enumerate(zip(in_chs, FEAT_MAP_DIM)):
            bound = 1.0 / np.sqrt(ic)
            params[f'W{i}'] = jax.random.uniform(ks[1 + 2 * i], (oc, ic), jnp.float32, -bound, bound)
            params[f'b{i}'] = jax.random.uniform(ks[2 + 2 * i], (oc,), jnp.float32, -bound, bound)
        return {'inp': inp, **params}
    _L0_rec_all = _L0_rec_setup()
    _L0_rec_in = {k: v for k, v in _L0_rec_all.items() if k in ('W0', 'b0', 'W1', 'b1', 'W2', 'b2')}
    del _L0_rec_all
    return {'dense_ctx': dense_ctx, 'ids': ids, 'tbl_0': tbl_0, 'tbl_1': tbl_1, 'tbl_2': tbl_2, 'tbl_3': tbl_3, 'tbl_4': tbl_4, 'tbl_5': tbl_5, 'tbl_6': tbl_6, 'tbl_7': tbl_7, 'tbl_8': tbl_8, 'tbl_9': tbl_9, 'tbl_10': tbl_10, 'tbl_11': tbl_11, 'tbl_12': tbl_12, 'tbl_13': tbl_13, 'tbl_14': tbl_14, 'tbl_15': tbl_15, 'tbl_16': tbl_16, 'tbl_17': tbl_17, 'tbl_18': tbl_18, 'tbl_19': tbl_19, 'tbl_20': tbl_20, 'tbl_21': tbl_21, 'tbl_22': tbl_22, 'tbl_23': tbl_23, 'tbl_24': tbl_24, 'tbl_25': tbl_25, 'tbl_26': tbl_26, 'tbl_27': tbl_27, 'tbl_28': tbl_28, 'tbl_29': tbl_29, 'tbl_30': tbl_30, 'tbl_31': tbl_31, 'W_top1': W_top1, 'b_top1': b_top1, 'W_top2': W_top2, 'b_top2': b_top2, 'W_top3': W_top3, 'L0_rec_W0': _L0_rec_in['W0'], 'L0_rec_b0': _L0_rec_in['b0'], 'L0_rec_W1': _L0_rec_in['W1'], 'L0_rec_b1': _L0_rec_in['b1'], 'L0_rec_W2': _L0_rec_in['W2'], 'L0_rec_b2': _L0_rec_in['b2']}

def reference(dense_ctx, ids, tbl_0, tbl_1, tbl_2, tbl_3, tbl_4, tbl_5, tbl_6, tbl_7, tbl_8, tbl_9, tbl_10, tbl_11, tbl_12, tbl_13, tbl_14, tbl_15, tbl_16, tbl_17, tbl_18, tbl_19, tbl_20, tbl_21, tbl_22, tbl_23, tbl_24, tbl_25, tbl_26, tbl_27, tbl_28, tbl_29, tbl_30, tbl_31, W_top1, b_top1, W_top2, b_top2, W_top3, L0_rec_W0, L0_rec_b0, L0_rec_W1, L0_rec_b1, L0_rec_W2, L0_rec_b2):
    import jax
    import jax.numpy as jnp

    def _L0_rec_ref(inp, W0, b0, W1, b1, W2, b2):
        import jax, jax.numpy as jnp
        import numpy as np
        B, NF, EMB = (256, 32, 64)
        FEAT_MAP_DIM = [128, 128, 128]
        nf = inp.shape[1]
        Ws, bs = ([W0, W1, W2], [b0, b1, b2])
        h = inp
        outs = []
        n_layers = len(Ws)
        for i, (W, b) in enumerate(zip(Ws, bs)):
            O, Hj = (W.shape[0], h.shape[1])
            Wr = W.reshape(O, Hj, nf)
            nxt = jnp.einsum('bjk,bzk,ojz->bok', h, inp, Wr) + b[None, :, None]
            if i != n_layers - 1:
                h, o = (nxt[:, :O // 2], nxt[:, O // 2:])
            else:
                o = nxt
            outs.append(o)
        out = jnp.concatenate(outs, axis=1)
        return jnp.sum(out, axis=2)
    e = jnp.stack([tbl_0[ids[:, 0]], tbl_1[ids[:, 1]], tbl_2[ids[:, 2]], tbl_3[ids[:, 3]], tbl_4[ids[:, 4]], tbl_5[ids[:, 5]], tbl_6[ids[:, 6]], tbl_7[ids[:, 7]], tbl_8[ids[:, 8]], tbl_9[ids[:, 9]], tbl_10[ids[:, 10]], tbl_11[ids[:, 11]], tbl_12[ids[:, 12]], tbl_13[ids[:, 13]], tbl_14[ids[:, 14]], tbl_15[ids[:, 15]], tbl_16[ids[:, 16]], tbl_17[ids[:, 17]], tbl_18[ids[:, 18]], tbl_19[ids[:, 19]], tbl_20[ids[:, 20]], tbl_21[ids[:, 21]], tbl_22[ids[:, 22]], tbl_23[ids[:, 23]], tbl_24[ids[:, 24]], tbl_25[ids[:, 25]], tbl_26[ids[:, 26]], tbl_27[ids[:, 27]], tbl_28[ids[:, 28]], tbl_29[ids[:, 29]], tbl_30[ids[:, 30]], tbl_31[ids[:, 31]]], axis=1)
    z = _L0_rec_ref(e, L0_rec_W0, L0_rec_b0, L0_rec_W1, L0_rec_b1, L0_rec_W2, L0_rec_b2)
    z = z.reshape(z.shape[0], -1)
    h = jnp.concatenate([z, dense_ctx], axis=1)
    h = jnp.maximum(h @ W_top1 + b_top1, 0.0)
    h = jnp.maximum(h @ W_top2 + b_top2, 0.0)
    y = h @ W_top3
    return y

_drawn_inputs = setup_inputs


def setup_inputs(seed=0):
    import zlib

    import numpy as np

    out = dict(_drawn_inputs(seed))
    spreads = {'b_top1': (0.0, 0.509), 'b_top2': (0.0, 0.1)}
    factors = {'tbl_0': 8.0,
     'tbl_1': 8.0,
     'tbl_2': 8.0,
     'tbl_3': 8.0,
     'tbl_4': 8.0,
     'tbl_5': 8.0,
     'tbl_6': 8.0,
     'tbl_7': 8.0,
     'tbl_8': 8.0,
     'tbl_9': 8.0,
     'tbl_10': 8.0,
     'tbl_11': 8.0,
     'tbl_12': 8.0,
     'tbl_13': 8.0,
     'tbl_14': 8.0,
     'tbl_15': 8.0,
     'tbl_16': 8.0,
     'tbl_17': 8.0,
     'tbl_18': 8.0,
     'tbl_19': 8.0,
     'tbl_20': 8.0,
     'tbl_21': 8.0,
     'tbl_22': 8.0,
     'tbl_23': 8.0,
     'tbl_24': 8.0,
     'tbl_25': 8.0,
     'tbl_26': 8.0,
     'tbl_27': 8.0,
     'tbl_28': 8.0,
     'tbl_29': 8.0,
     'tbl_30': 8.0,
     'tbl_31': 8.0,
     'L0_rec_W0': 3.111,
     'L0_rec_W1': 8.0,
     'L0_rec_W2': 8.0}
    for name, (base, spread) in spreads.items():
        noise = np.random.default_rng([zlib.crc32(name.encode()), seed]).standard_normal(out[name].shape)
        drawn = base * np.exp(spread * noise) if base else spread * noise
        out[name] = jnp.asarray(drawn.astype(out[name].dtype))
    for name, factor in factors.items():
        out[name] = (out[name] * factor).astype(out[name].dtype)
    return out
```

```python
from contextlib import ExitStack

import concourse.bass as bass
from concourse import mybir

FP32 = mybir.dt.float32
INT32 = mybir.dt.int32
ALU = mybir.AluOpType
ACT = mybir.ActivationFunctionType

B, NF, K = 512, 32, 64
C = 64
P = 128
DENSE = 16
GROUPS = B // P
TILES = 16
STEPS = B // 2 // TILES
QUARTERS = 4
FQ = NF // QUARTERS
PAIRS = NF * (NF + 1) // 2
COLS = PAIRS + NF
HALFCOLS = COLS // 2
CHUNKS = [(c, min(P, PAIRS - c)) for c in range(0, PAIRS, P)]
NCH = len(CHUNKS)
LOT = 4
BANK = 512
G1COLS, G0COLS = TILES * NF, 2 * (TILES // 4) * NF
KEEP = G1COLS + G0COLS
SLOTS = 4
FIRST_LOOKUPS = STEPS - QUARTERS


def pair_at(z):
    return 32 * z if z < 16 else 33 * (31 - z) + 1


def g2_segments():
    out = []
    for z in range(NF):
        low = min(z, 16)
        if low:
            out.append((z, pair_at(0) + z, 32, 0, low))
        if z > 16:
            out.append((z, pair_at(16) + z, -33, 16, z - 16))
        out.append((z, pair_at(z) + z, 1, z, NF - z))
    return out


def dlrm_tower(nc, dense_ctx, ids, tables, W_top1, b_top1, W_top2, b_top2, W_top3,
               W0, b0, W1, b1, W2, b2, y_out):
    ctx = ExitStack()
    with ctx:
        def sb(name, shape, dt=FP32):
            return ctx.enter_context(nc.sbuf_tensor(name, shape, dt))

        def ps(name, shape):
            return ctx.enter_context(nc.psum_tensor(name, shape, FP32))

        def sem(name):
            return ctx.enter_context(nc.semaphore(name))

        XCOLS, PCOLS = GROUPS * NF * K, TILES * COLS
        xp = sb("xp", [P, XCOLS + PCOLS])
        XT = xp[:, 0:XCOLS].rearrange("p (g z s) -> p g z s", g=GROUPS, z=NF)
        PX = xp[:, XCOLS:XCOLS + PCOLS].rearrange("p (t c) -> p t c", t=TILES)
        T_flat = sb("T_sb", [P, TILES * COLS])
        T_sb = T_flat[:, :].rearrange("p (t c) -> p t c", t=TILES)
        PT = sb("PT", [P, SLOTS, BANK])
        E_q = sb("E_q", [P, FQ, K])
        H_sb = sb("H_sb", [P, 2, BANK])
        H_bd = sb("H_bd", [P, TILES, P])
        W1_bd = sb("W1_bd", [P, NF, P])
        b1_bd = sb("b1_bd", [P, P])
        W0T = sb("W0T", [P, NCH, C])
        G2_flat = sb("G2_sb", [P, NF * B // 2])
        G2_sb = G2_flat[:, :].rearrange("p (y s) -> p y s", y=NF)
        kept = sb("kept", [P, KEEP])
        ident = sb("ident", [P, P])
        ids_0 = sb("ids_0", [P, NF], INT32)
        ids_g = sb("ids_g", [P, NF], INT32)
        Wt1 = sb("Wt1", [P, 2, 512])
        Wt1d = sb("Wt1d", [DENSE, 512])
        Wt2 = sb("Wt2", [P, 4, 256])
        Wt3 = sb("Wt3", [P, 2])
        dT = sb("dT", [DENSE, B])
        b0_col = sb("b0_col", [P, 1])
        zb = sb("zb", [P, 2])
        zb64 = sb("zb64", [P, 2])
        bt1 = sb("bt1", [P, 4])
        bt2 = sb("bt2", [P, 2])

        raw = XCOLS
        W0_raw = xp[:, raw:raw + 1024].rearrange("p (i z) -> p i z", z=NF)
        W1_raw = xp[:, raw + 1024:raw + 3072].rearrange("p (i z) -> p i z", z=NF)
        W2_raw = xp[:, raw + 3072:raw + 5120].rearrange("p (i z) -> p i z", z=NF)
        W0_sym = xp[0:C, raw + 5120:raw + 5120 + PAIRS]
        d_raw = xp[:, raw + 5888:raw + 5888 + GROUPS * DENSE].rearrange("p (g d) -> p g d", g=GROUPS)
        E_0 = G2_flat[:, 0:NF * K].rearrange("p (z k) -> p z k", z=NF)
        W2T_new = T_flat[:, 0:4096].rearrange("p (y o) -> p y o", y=NF)
        W0z_new = T_flat[:, 4096:6144].rearrange("p (y o) -> p y o", y=NF)
        W1h_new = T_flat[:, 6144:8192].rearrange("p (z o) -> p z o", z=NF)
        W2T = xp[:, 0:4096].rearrange("p (y o) -> p y o", y=NF)
        G01 = xp[:, 4096:4096 + STEPS * KEEP].rearrange("p (n c) -> p n c", n=STEPS)
        G1_all = G01[:, :, 0:G1COLS].rearrange("p n (z t) -> p n z t", z=NF)
        G0_all = G01[:, :, G1COLS:KEEP].rearrange("p n (h y q) -> p n h y q", h=2, y=NF)
        W0z = PT[:, :, :].rearrange("p a b -> p (a b)").rearrange("p (y o) -> p y o", y=NF)
        W1h = H_bd[:, :, :].rearrange("p a b -> p (a b)").rearrange("p (z o) -> p z o", z=NF)
        zA = T_flat[:, 0:512]
        zB = T_flat[:, 512:1024]
        h1 = T_flat[:, 1024:3072].rearrange("p (m b) -> p m b", m=4)
        h2 = T_flat[:, 3072:4096].rearrange("p (m b) -> p m b", m=2)
        y_sb = T_flat[0:1, 4096:4608]

        weights_out = nc.dram_tensor("weights_out", [P, 8192], FP32, kind="Internal").ap()
        kept_out = nc.dram_tensor("kept_out", [STEPS, P, KEEP], FP32, kind="Internal").ap()

        psT = ps("psT", [P, 4, BANK])
        psP = ps("psP", [P, 2, BANK])
        psH = ps("psH", [P, BANK])
        psG = ps("psG", [P, BANK])

        small_in = sem("small_in")
        w0_in, w1_in, w2_in = sem("w0_in"), sem("w1_in"), sem("w2_in")
        ids0_in, idsg_in = sem("ids0_in"), sem("idsg_in")
        zeroed = sem("zeroed")
        w0_sym = sem("w0_sym")
        zb_ready = sem("zb_ready")
        w_tr = sem("w_tr")
        w_evac = sem("w_evac")
        first_rows = [sem(f"first_rows{q}") for q in range(QUARTERS)]
        rows_in = sem("rows_in")
        lookups_begun = sem("lookups_begun")
        x_tr = sem("x_tr")
        x_evac = sem("x_evac")
        px_ready = sem("px_ready")
        p_tr = sem("p_tr")
        p_evac = sem("p_evac")
        p_used = sem("p_used")
        h_evac = sem("h_evac")
        h_tr = sem("h_tr")
        hbd_ready = sem("hbd_ready")
        t_ready = sem("t_ready")
        t_evac = sem("t_evac")
        g0_ready = sem("g0_ready")
        g0_evac = sem("g0_evac")
        g1_kept = sem("g1_kept")
        kept_sent = sem("kept_sent")
        g2_ready = sem("g2_ready")
        g2_evac = sem("g2_evac")
        w2t_in, w0z_in, w1h_in, g01_in = sem("w2t_in"), sem("w0z_in"), sem("w1h_in"), sem("g01_in")
        z0_ready, z1_ready, z2_ready = sem("z0_ready"), sem("z1_ready"), sem("z2_ready")
        z_evac = sem("z_evac")
        h1_ready, h1_evac = sem("h1_ready"), sem("h1_evac")
        h2_ready, h2_evac = sem("h2_ready"), sem("h2_evac")
        y_ready, y_evac, y_sent = sem("y_ready"), sem("y_evac"), sem("y_sent")

        LOTS = 2 * 2 * NCH
        N_ZERO = 3
        W_BANKS = NF // 4 + NF // 8 + NF // 4 + 2
        SMALL = 13

        block = ctx.enter_context(nc.Block())

        @block.sync
        def _(sp):
            sp.dma_start(ids_0[:, :], ids[0:P, :]).then_inc(ids0_in, 16)
            sp.dma_start(W0_raw.rearrange("p i z -> p (i z)"), W0).then_inc(w0_in, 16)
            sp.dma_start(W1_raw.rearrange("p i z -> p (i z)"), W1).then_inc(w1_in, 16)
            sp.dma_start(W2_raw.rearrange("p i z -> p (i z)"), W2).then_inc(w2_in, 16)
            sp.dma_start(d_raw, dense_ctx.rearrange("(g p) d -> p g d", p=P)).then_inc(w2_in, 16)
            sp.dma_start(Wt1[:, :, :], W_top1[0:2 * P, :].rearrange("(a p) n -> p a n", p=P)).then_inc(small_in, 16)
            sp.dma_start(Wt1d[:, :], W_top1[2 * P:2 * P + DENSE, :]).then_inc(small_in, 16)
            sp.dma_start(Wt2[:, :, :], W_top2.rearrange("(a p) n -> p a n", p=P)).then_inc(small_in, 16)
            sp.dma_start(Wt3[:, :], W_top3.rearrange("(a p) o -> p (a o)", p=P),
                         allow_slow_non_contiguous=True).then_inc(small_in, 16)
            sp.dma_start(bt1[:, :], b_top1.rearrange("(m p) -> p m", p=P),
                         allow_slow_non_contiguous=True).then_inc(small_in, 16)
            sp.dma_start(bt2[:, :], b_top2.rearrange("(m p) -> p m", p=P),
                         allow_slow_non_contiguous=True).then_inc(small_in, 16)
            for lot in range(2):
                sp.dma_start(b0_col[C * lot:C * lot + C, :], b0[0:C].unsqueeze(1)).then_inc(small_in, 16)
            sp.dma_start(zb[0:C, 0:1], b0[C:P].unsqueeze(1)).then_inc(small_in, 16)
            sp.dma_start(zb[C:P, 0:1], b1[C:P].unsqueeze(1)).then_inc(small_in, 16)
            sp.dma_start(zb[:, 1:2], b2.unsqueeze(1)).then_inc(small_in, 16)
            sp.wait_ge(zeroed, N_ZERO)
            for h in range(2):
                sp.dma_start(b1_bd[C * h:C * h + C, C * h:C * h + C],
                             b1[0:C].unsqueeze(0).broadcast_to([C, C])).then_inc(small_in, 16)
            sp.wait_ge(w_evac, W_BANKS)
            sp.dma_start(weights_out, T_flat[:, 0:8192]).then_inc(kept_sent, 16)

            with sp.Fori(0, STEPS) as n:
                sp.wait_ge(g1_kept, n + 2)
                sp.wait_ge(g0_evac, n + 2)
                sp.dma_start(kept_out[bass.ds(n, 1), :, :].rearrange("a p c -> (a p) c"), kept[:, :])\
                  .then_inc(kept_sent, 16)
            sp.wait_ge(kept_sent, 16)
            sp.wait_ge(p_used, LOTS // 2 * STEPS)
            sp.dma_start(W0z.rearrange("p y o -> p (y o)"), weights_out[:, 4096:6144]).then_inc(w0z_in, 16)
            sp.wait_ge(px_ready, STEPS)
            sp.dma_start(W2T.rearrange("p y o -> p (y o)"), weights_out[:, 0:4096]).then_inc(w2t_in, 16)
            sp.wait_ge(g0_ready, STEPS)
            sp.dma_start(W1h.rearrange("p z o -> p (z o)"), weights_out[:, 6144:8192]).then_inc(w1h_in, 16)
            sp.wait_ge(kept_sent, 16 * (STEPS + 1))
            sp.dma_start(G01, kept_out.rearrange("n p c -> p n c")).then_inc(g01_in, 16)

            sp.wait_ge(y_evac, 1)
            sp.dma_start(y_out.rearrange("(g h s) o -> o h g s", g=GROUPS, h=2),
                         y_sb.rearrange("o (h g s) -> o h g s", h=2, g=GROUPS)).then_inc(y_sent, 16)
            sp.wait_ge(y_sent, 16)

        @block.gpsimd
        def _(pool):
            nc.gpsimd.memset(ident[:, :], 0.0).then_inc(zeroed, 1)
            nc.gpsimd.memset(b1_bd[:, :], 0.0).then_inc(zeroed, 1)
            nc.gpsimd.memset(H_bd[:, :, :], 0.0).then_inc(zeroed, 1)
            pool.wait_ge(zeroed, N_ZERO)
            nc.gpsimd.affine_select(out=ident[:, :], in_=ident[:, :], compare_op=ALU.not_equal, fill=1.0,
                                    base=0, pattern=[[-1, P]], channel_multiplier=1).then_inc(zeroed, 1)
            pool.wait_ge(ids0_in, 16)
            for z in range(NF):
                nc.gpsimd.indirect_dma_start(
                    out=E_0[:, z, :], out_offset=None, in_=tables[z],
                    in_offset=bass.IndirectOffsetOnAxis(ap=ids_0[:, z:z + 1], axis=0),
                ).then_inc(first_rows[z // FQ], 16)
            with pool.Fori(1, GROUPS) as g:
                pool.wait_ge(x_tr, QUARTERS * g)
                pool.dma_start(ids_g[:, :], ids[bass.ds(g * P, P), :]).then_inc(idsg_in, 16)
                pool.wait_ge(idsg_in, 16 * g)
                for q in range(QUARTERS):
                    pool.wait_ge(x_tr, QUARTERS * g + q)
                    pool.sem_inc(lookups_begun, 1)
                    for z in range(FQ * q, FQ * q + FQ):
                        nc.gpsimd.indirect_dma_start(
                            out=E_q[:, z - FQ * q, :], out_offset=None, in_=tables[z],
                            in_offset=bass.IndirectOffsetOnAxis(ap=ids_g[:, z:z + 1], axis=0),
                        ).then_inc(rows_in, 16)

        @block.tensor
        def _(pe):
            mm = nc.tensor.matmul

            def transposed_to(out, rows, first, eye):
                n = rows.shape[1]
                return mm(out[first:first + n], rows, eye, start=True, stop=True, tile_position=(0, first))

            def x_transposes(rows, bank):
                for a in range(FQ):
                    for h in range(2):
                        last = transposed_to(psP[:, bank, K * a:K * a + K], rows[:, a, :], C * h,
                                             ident[:, C * h:C * h + C])
                last.then_inc(x_tr, 1)

            def lot_transposes(m, pr, c, lot):
                k = (pr * NCH + c) * 2 + lot
                c0, cn = CHUNKS[c]
                if k >= 2:
                    pe.wait_ge(p_evac, LOTS * m + k - 1)
                for a in range(LOT):
                    tile = (2 * pr + lot) * LOT + a
                    last = nc.tensor.transpose(psP[0:cn, k % 2, P * a:P * a + P],
                                               PX[:, tile, c0:c0 + cn], ident[:, :])
                last.then_inc(p_tr, 1)

            def h_matmuls(m, pr, c):
                cn = CHUNKS[c][1]
                k = (pr * NCH + c) * 2
                pe.wait_ge(p_evac, LOTS * m + k + 2)
                for lot in range(2):
                    last = mm(psH[C * lot:C * lot + C, :], W0T[0:cn, c, :], PT[0:cn, (k + lot) % SLOTS, :],
                              start=(c == 0), stop=(c == NCH - 1), tile_position=(0, C * lot))
                last.then_inc(p_used, 1)

            def h_transposes(m, pr):
                pe.wait_ge(h_evac, 2 * m + pr + 1)
                for a in range(LOT):
                    last = nc.tensor.transpose(psT[:, pr, P * a:P * a + P], H_sb[:, pr, P * a:P * a + P],
                                               ident[:, :])
                last.then_inc(h_tr, 1)

            def next_h(m, g2):
                for pr in range(2):
                    for c in range(NCH):
                        for lot in range(2):
                            lot_transposes(m, pr, c, lot)
                        if c == 0 and pr == 1:
                            h_matmuls(m, 0, NCH - 1)
                            g2(2)
                            h_transposes(m, 0)
                        if c == 1 and pr == 1:
                            h_matmuls(m, 1, 0)
                        elif c:
                            h_matmuls(m, pr, c - 1)
                        g2(5)
                h_matmuls(m, 1, NCH - 1)
                g2(3)
                h_transposes(m, 1)

            count = [0]

            def next_bank():
                k = count[0]
                count[0] += 1
                if k >= 4:
                    pe.wait_ge(w_evac, k - 3)
                return psT[:, k % 4, :]

            pe.wait_ge(zeroed, N_ZERO + 1)
            pe.wait_ge(w1_in, 16)
            for z in range(0, NF, 4):
                bank = next_bank()
                for a in range(4):
                    for h in range(2):
                        last = transposed_to(bank[:, P * a:P * a + P], W1_raw[:, 0:C, z + a], C * h, ident[:, :])
                last.then_inc(w_tr, 1)
            pe.wait_ge(w0_in, 16)
            for y in range(0, NF, 8):
                bank = next_bank()
                for a in range(8):
                    for j in range(4):
                        last = transposed_to(bank[:, C * a:C * a + C], W0_raw[:, :, y + a], NF * j, ident[:, C:P])
                last.then_inc(w_tr, 1)
            pe.wait_ge(w2_in, 32)
            for y in range(0, NF, 4):
                bank = next_bank()
                for a in range(4):
                    for h in range(2):
                        last = transposed_to(bank[:, P * a:P * a + P], W2_raw[:, 0:C, y + a], C * h, ident[:, :])
                last.then_inc(w_tr, 1)
            bank = next_bank()
            for g in range(GROUPS):
                last = nc.tensor.transpose(bank[0:DENSE, P * g:P * g + P], d_raw[:, g, :], ident[:, :])
            last.then_inc(w_tr, 1)
            pe.wait_ge(w0_sym, 3)
            bank = next_bank()
            for c, (c0, cn) in enumerate(CHUNKS):
                last = nc.tensor.transpose(bank[0:cn, C * c:C * c + C], W0_sym[:, c0:c0 + cn], ident[0:C, 0:C])
            last.then_inc(w_tr, 1)

            for q in range(QUARTERS):
                pe.wait_ge(first_rows[q], 16 * FQ)
                if q >= 2:
                    pe.wait_ge(x_evac, q - 1)
                x_transposes(E_0[:, FQ * q:FQ * q + FQ, :], q % 2)

            pe.wait_ge(w_evac, W_BANKS)
            pe.wait_ge(px_ready, 1)
            next_h(0, lambda count: None)
            pe.wait_ge(small_in, 16 * (SMALL))

            pe.sem_inc(g2_ready, 1)

            def step(n, lookups, last_step):
                if lookups:
                    pe.wait_ge(rows_in, 16 * FQ * (n + 1))
                    pe.wait_ge(p_evac, LOTS * (n + 1))
                    x_transposes(E_q, 1)
                pe.wait_ge(hbd_ready, 4 * (n + 1))
                pe.wait_ge(g0_evac, n + 1)
                for t in range(TILES):
                    if t >= 2:
                        pe.wait_ge(t_evac, TILES * n + t - 1)
                    for a in range(2):
                        last = mm(psT[:, 2 * (t % 2) + a, 0:HALFCOLS], H_bd[:, t, :],
                                  PX[:, t, HALFCOLS * a:HALFCOLS * (a + 1)], start=True, stop=True)
                    last.then_inc(t_ready, 1)
                segments = g2_segments()
                done = [0]
                G = psG[:, :].rearrange("p (t y) -> p t y", y=NF)

                def g2(count):
                    for z, col, by, y, cnt in segments[done[0]:done[0] + count]:
                        end = col + by * cnt if by > 0 else col + by * (cnt - 1) - 1
                        last = mm(G[:, :, y:y + cnt], W1_bd[:, z, :], T_sb[:, :, col:min(end, COLS):by],
                                  start=False, stop=(done[0] == len(segments) - 1))
                        done[0] += 1
                        if done[0] == len(segments):
                            last.then_inc(g2_ready, 1)

                pe.wait_ge(g2_evac, n + 1)
                mm(psG[:, :], b1_bd[:, :], PX[:, :, PAIRS:COLS], start=True, stop=False)
                pe.wait_ge(t_evac, TILES * (n + 1))
                g2(1)
                for t in range(TILES):
                    for h in range(2):
                        x = PX[C * h:C * h + C, t, PAIRS:COLS]
                        j, q = t % 4, t // 4
                        last = mm(psT[NF * j:NF * j + NF, 2 + h, NF * q:NF * q + NF], x, x,
                                  start=True, stop=True, tile_position=(C * h, NF * j))
                last.then_inc(g0_ready, 1)

                g2(26)
                if not last_step:
                    pe.wait_ge(px_ready, n + 2)
                    if lookups:
                        pe.wait_ge(x_evac, QUARTERS + n + 1)
                    next_h(n + 1, g2)
                g2(len(segments))

            with pe.Fori(0, FIRST_LOOKUPS) as n:
                step(n, True, False)
            with pe.Fori(FIRST_LOOKUPS, STEPS - 1) as n:
                step(n, False, False)
            step(STEPS - 1, False, True)

            pe.wait_ge(w0z_in, 16)
            pe.wait_ge(w1h_in, 16)
            pe.wait_ge(g01_in, 16)
            pe.wait_ge(t_evac, TILES * STEPS)
            for z in range(NF):
                for h in range(2):
                    for j in (2 * h, 2 * h + 1):
                        r = slice(NF * j, NF * j + NF)
                        last0 = mm(psT[0:C, j, 0:P].rearrange("p (h n q) -> p n h q", h=2, n=STEPS),
                                   W0z[r, z, :], G0_all[r, :, :, z, :],
                                   start=(z == 0), stop=(z == NF - 1), tile_position=(NF * j, 0))
                    r = slice(C * h, C * h + C)
                    last1 = mm(psP[C:P, h, 0:256].rearrange("p (n t) -> p n t", n=STEPS),
                               W1h[r, z, :], G1_all[r, :, z, :],
                               start=(z == 0), stop=(z == NF - 1), tile_position=(C * h, C))
            last0.then_inc(z0_ready, 1)
            last1.then_inc(z1_ready, 1)
            pe.wait_ge(w2t_in, 16)
            pe.wait_ge(g2_evac, STEPS + 1)
            for y in range(NF):
                for h in range(2):
                    r = slice(C * h, C * h + C)
                    last = mm((psH, psG)[h][:, 0:256], W2T[r, y, :], G2_sb[r, y, :],
                              start=(y == 0), stop=(y == NF - 1), tile_position=(C * h, 0))
            last.then_inc(z2_ready, 1)

            pe.wait_ge(z_evac, 8)
            for m in range(4):
                cols = slice(P * m, P * m + P)
                mm(psT[:, m, :], Wt1[:, 0, cols], zA, start=True, stop=False)
                mm(psT[:, m, :], Wt1[:, 1, cols], zB, start=False, stop=False)
                mm(psT[:, m, :], Wt1d[:, cols], dT[:, :], start=False, stop=True).then_inc(h1_ready, 1)
            for a in range(4):
                pe.wait_ge(h1_evac, a + 1)
                for m in range(2):
                    last = mm(psP[:, m, :], Wt2[:, a, P * m:P * m + P], h1[:, a, :],
                              start=(a == 0), stop=(a == 3))
            last.then_inc(h2_ready, 1)
            pe.wait_ge(h2_evac, 2)
            for a in range(2):
                last = mm(psH[0:1, :], Wt3[:, a:a + 1], h2[:, a, :], start=(a == 0), stop=(a == 1))
            last.then_inc(y_ready, 1)

        @block.scalar
        def _(act):
            copy = nc.scalar.copy

            act.wait_ge(zeroed, N_ZERO)
            act.wait_ge(w0_sym, 1)
            k = 0
            for z in range(0, NF, 4):
                bank = psT[:, k % 4, :].rearrange("p (a o) -> p a o", a=4)
                act.wait_ge(w_tr, k + 1)
                for h in range(2):
                    copy(W1_bd[C * h:C * h + C, z:z + 4, C * h:C * h + C], bank[C * h:C * h + C, :, 0:C])
                copy(W1h_new[:, z:z + 4, :], bank[:, :, C:P]).then_inc(w_evac, 1)
                k += 1
            for y in range(0, NF, 8):
                act.wait_ge(w_tr, k + 1)
                copy(W0z_new[:, y:y + 8, :], psT[:, k % 4, :].rearrange("p (a o) -> p a o", a=8))\
                    .then_inc(w_evac, 1)
                k += 1
            for y in range(0, NF, 4):
                act.wait_ge(w_tr, k + 1)
                copy(W2T_new[:, y:y + 4, :], psT[:, k % 4, :].rearrange("p (a o) -> p a o", a=4))\
                    .then_inc(w_evac, 1)
                k += 1
            act.wait_ge(w_tr, k + 1)
            copy(dT[:, :].rearrange("d (h g s) -> d g h s", h=2, g=GROUPS),
                 psT[0:DENSE, k % 4, :].rearrange("d (g h s) -> d g h s", g=GROUPS, h=2)).then_inc(w_evac, 1)
            k += 1
            act.wait_ge(w_tr, k + 1)
            copy(W0T[:, 0:NCH - 1, :], psT[:, k % 4, 0:C * (NCH - 1)].rearrange("p (c i) -> p c i", i=C))
            cn = CHUNKS[-1][1]
            copy(W0T[0:cn, NCH - 1, :], psT[0:cn, k % 4, C * (NCH - 1):C * NCH]).then_inc(w_evac, 1)
            act.wait_ge(small_in, 16 * (SMALL))

            def lot_copies(m, pr, c):
                cn = CHUNKS[c][1]
                for lot in range(2):
                    k = (pr * NCH + c) * 2 + lot
                    act.wait_ge(p_tr, LOTS * m + k + 1)
                    if not (isinstance(m, int) and m == 0 and k < SLOTS):
                        act.wait_ge(p_used, LOTS // 2 * m + k // 2 - 1)
                    copy(PT[0:cn, k % SLOTS, :], psP[0:cn, k % 2, :]).then_inc(p_evac, 1)

            def h_copy(m, pr):
                act.wait_ge(p_used, LOTS // 2 * m + NCH * (pr + 1))
                nc.scalar.activation(H_sb[:, pr, :], psH[:, :], ACT.Identity, bias=b0_col[:, :])\
                    .then_inc(h_evac, 1)

            def h_blocks(m, pr):
                act.wait_ge(h_tr, 2 * m + pr + 1)
                for h in range(2):
                    r = slice(C * h, C * h + C)
                    out = H_bd[r, 2 * LOT * pr:2 * LOT * (pr + 1), C * h:C * h + C]
                    copy(out.rearrange("p (l a) i -> p l a i", l=2),
                         psT[r, pr, :].rearrange("p (a l i) -> p l a i", l=2, i=C)).then_inc(hbd_ready, 1)

            def next_h(m):
                for pr in range(2):
                    for c in range(NCH):
                        lot_copies(m, pr, c)
                        if c == 0 and pr == 1:
                            h_copy(m, 0)
                            h_blocks(m, 0)
                h_copy(m, 1)
                h_blocks(m, 1)

            next_h(0)
            act.wait_ge(kept_sent, 16)
            act.sem_inc(g2_evac, 1)

            def step(n, last_step):
                act.wait_ge(g2_ready, n + 1)
                act.wait_ge(g1_kept, n + 1)
                for t in range(TILES):
                    act.wait_ge(t_ready, TILES * n + t + 1)
                    copy(T_sb[:, t, :].rearrange("p (a c) -> p a c", a=2),
                         psT[:, 2 * (t % 2):2 * (t % 2) + 2, 0:HALFCOLS]).then_inc(t_evac, 1)
                if not last_step:
                    next_h(n + 1)
                act.wait_ge(g2_ready, n + 2)
                copy(G2_sb[:, :, bass.ds(n * TILES, TILES)],
                     psG[:, :].rearrange("p (t y) -> p y t", y=NF)).then_inc(g2_evac, 1)

            with act.Fori(0, STEPS - 1) as n:
                step(n, False)
            step(STEPS - 1, True)

            act.wait_ge(zb_ready, 1)
            act.wait_ge(z0_ready, 1)
            for j in range(4):
                nc.scalar.activation(zA[0:C, j:B:4], psT[0:C, j, 0:P], ACT.Identity,
                                     bias=zb64[0:C, 0:1]).then_inc(z_evac, 1)
            act.wait_ge(z1_ready, 1)
            for h in range(2):
                nc.scalar.activation(zA[C:P, 256 * h:256 * h + 256], psP[C:P, h, 0:256], ACT.Identity,
                                     bias=zb64[C:P, 0:1]).then_inc(z_evac, 1)
            act.wait_ge(z2_ready, 1)
            for h in range(2):
                nc.scalar.activation(zB[:, 256 * h:256 * h + 256], (psH, psG)[h][:, 0:256], ACT.Identity,
                                     bias=zb64[:, 1:2]).then_inc(z_evac, 1)
            for m in range(4):
                act.wait_ge(h1_ready, m + 1)
                nc.scalar.activation(h1[:, m, :], psT[:, m, :], ACT.Relu, bias=bt1[:, m:m + 1])\
                    .then_inc(h1_evac, 1)
            act.wait_ge(h2_ready, 1)
            for m in range(2):
                nc.scalar.activation(h2[:, m, :], psP[:, m, :], ACT.Relu, bias=bt2[:, m:m + 1])\
                    .then_inc(h2_evac, 1)
            act.wait_ge(y_ready, 1)
            copy(y_sb, psH[0:1, :]).then_inc(y_evac, 1)

        @block.vector
        def _(dve):
            tt = nc.vector.tensor_tensor
            nc.vector.memset(W1_bd[:, :, :], 0.0).then_inc(w0_sym, 1)
            dve.wait_ge(w0_in, 16)
            for z in range(NF - 1):
                at = pair_at(z)
                tt(W0_sym[:, at + z + 1:at + NF], W0_raw[0:C, z, z + 1:NF], W0_raw[0:C, z + 1:NF, z], ALU.add)
            flat = W0_raw[0:C, :, :].rearrange("p i z -> p (i z)")
            nc.vector.tensor_copy(W0_sym[:, 0:33 * 15 + 1:33], flat[:, 0:33 * 15 + 1:33]).then_inc(w0_sym, 1)
            last_at = pair_at(31) + 31
            nc.vector.tensor_copy(W0_sym[:, last_at:last_at + 32 * 15 + 1:32],
                                  flat[:, 33 * 31:33 * 15:-33]).then_inc(w0_sym, 1)
            dve.wait_ge(small_in, 16 * (SMALL))
            nc.vector.tensor_scalar_mul(zb64[:, :], zb[:, :], float(K)).then_inc(zb_ready, 1)

            def x_copy(bank, out):
                nc.vector.tensor_copy(out, psP[:, bank, :].rearrange("p (a s) -> p a s", a=FQ)).then_inc(x_evac, 1)

            def products(xt):
                for z in range(NF):
                    at = pair_at(z)
                    tt(PX[:, :, at + z:at + NF], xt(z, NF).rearrange("p z s -> p s z"),
                       xt(z, z + 1).rearrange("p z s -> p s z").broadcast_to([P, TILES, NF - z]), ALU.mult)
                nc.vector.tensor_copy(PX[:, :, PAIRS:COLS], xt(0, NF).rearrange("p z s -> p s z"))\
                    .then_inc(px_ready, 1)

            for q in range(QUARTERS):
                dve.wait_ge(x_tr, q + 1)
                x_copy(q % 2, XT[:, 0, FQ * q:FQ * q + FQ, :])
            dve.wait_ge(x_evac, QUARTERS)
            dve.sem_inc(g0_evac, 1)
            dve.sem_inc(g1_kept, 1)
            dve.wait_ge(w_tr, W_BANKS)
            products(lambda a, b: XT[:, 0, a:b, 0:TILES])

            X_rows = xp[:, 0:XCOLS].rearrange("p (u s) -> p u s", s=K)

            def keep(n):
                dve.wait_ge(t_evac, TILES * (n + 1))
                dve.wait_ge(kept_sent, 16 * (n + 1))
                nc.vector.tensor_copy(kept[:, 0:G1COLS].rearrange("p (z t) -> p t z", z=NF),
                                      T_sb[:, :, PAIRS:COLS]).then_inc(g1_kept, 1)
                for h in range(2):
                    c0 = G1COLS + h * G0COLS // 2
                    last = nc.vector.tensor_copy(
                        kept[:, c0:c0 + G0COLS // 2].rearrange("p (y q) -> p q y", y=NF),
                        psT[:, 2 + h, 0:G0COLS // 2].rearrange("p (q y) -> p q y", y=NF))
                last.then_inc(g0_evac, 1)

            def step(g, q, n, lookups):
                if lookups:
                    dve.wait_ge(x_tr, QUARTERS + n + 1)
                    x_copy(1, X_rows[:, bass.ds((g + 1) * NF + q * FQ, FQ), :])
                    dve.wait_ge(x_evac, QUARTERS + n + 1)
                dve.wait_ge(g0_ready, n + 1)
                if q < QUARTERS - 1:
                    products(lambda a, b: X_rows[:, bass.ds(g * NF + a, b - a), TILES * (q + 1):TILES * (q + 2)])
                else:
                    products(lambda a, b: X_rows[:, bass.ds((g + 1) * NF + a, b - a), 0:TILES])
                keep(n)

            with dve.Fori(0, GROUPS - 1) as g:
                for q in range(QUARTERS):
                    step(g, q, QUARTERS * g + q, True)
            for q in range(QUARTERS - 1):
                step(GROUPS - 1, q, QUARTERS * (GROUPS - 1) + q, False)
            dve.wait_ge(g0_ready, STEPS)
            keep(STEPS - 1)


_TABLES = [f"tbl_{f}" for f in range(NF)]
_INS = ["dense_ctx", "ids", *_TABLES, "W_top1", "b_top1", "W_top2", "b_top2", "W_top3",
        "L0_rec_W0", "L0_rec_b0", "L0_rec_W1", "L0_rec_b1", "L0_rec_W2", "L0_rec_b2"]


def kernel(**inputs):
    import numpy as _np
    import concourse.bacc as _bacc
    from concourse import mybir as _mybir
    from concourse.bass_utils import run_bass_kernel_spmd as _run

    nc = _bacc.Bacc("TRN2", target_bir_lowering=False, num_devices=1)
    arrays, aps = {}, {}
    for name in _INS:
        a = _np.ascontiguousarray(inputs[name])
        arrays[f"in_{name}"] = a
        aps[name] = nc.dram_tensor(f"in_{name}", a.shape, _mybir.dt.from_np(a.dtype), kind="ExternalInput").ap()
    y = nc.dram_tensor("y", [B, 1], _mybir.dt.float32, kind="ExternalOutput").ap()
    dlrm_tower(nc, aps["dense_ctx"], aps["ids"], [aps[t] for t in _TABLES],
               aps["W_top1"], aps["b_top1"], aps["W_top2"], aps["b_top2"], aps["W_top3"],
               aps["L0_rec_W0"], aps["L0_rec_b0"], aps["L0_rec_W1"], aps["L0_rec_b1"],
               aps["L0_rec_W2"], aps["L0_rec_b2"], y)
    r = _run(nc, [arrays], core_ids=[0])
    return r.results[0]["y"]
```

```python
from contextlib import ExitStack

import concourse.bass as bass
from concourse import mybir

FP32 = mybir.dt.float32
INT32 = mybir.dt.int32
ALU = mybir.AluOpType
ACT = mybir.ActivationFunctionType

B, NF, K = 512, 32, 64
C = 64
P = 128
DENSE = 16
BANK = 512
GROUPS = B // P
TILES = 8
SMP = 2 * TILES
STEPS = B // SMP
IN_GROUP = P // SMP
QUARTERS = 4
FQ = NF // QUARTERS
PAIRS_OF_STEPS = STEPS // 2
LOOKUP_PAIRS = PAIRS_OF_STEPS - QUARTERS
PF = NF // 2
E8 = PF // 2
TOP, LOW, CROSS = E8 * PF, E8 * E8, PF * PF
TOP_A = NF
LOW_A = TOP_A + TOP
CR = LOW_A + LOW
TOP_B = CR + CROSS
LOW_B = TOP_B + TOP
X_A2 = LOW_B + LOW
COLS = X_A2 + PF
PAIRCOLS = X_A2 - TOP_A
TW = PF + TOP + LOW + CROSS
A_FROM, B_FROM = PF, CR
NCH = PAIRCOLS // P
LOT = 4
LOTS = 2 * NCH
SLOTS = 4
G1COLS, G0COLS = PF * SMP, NF * SMP // 4
KEEP = G1COLS + G0COLS


def dlrm_tower(nc, dense_ctx, ids, tables, W_top1, b_top1, W_top2, b_top2, W_top3,
               W0, b0, W1, b1, W2, b2, y_out):
    ctx = ExitStack()
    with ctx:
        def sb(name, shape, dt=FP32):
            return ctx.enter_context(nc.sbuf_tensor(name, shape, dt))

        def ps(name, shape):
            return ctx.enter_context(nc.psum_tensor(name, shape, FP32))

        def sem(name):
            return ctx.enter_context(nc.semaphore(name))

        XCOLS, PCOLS = GROUPS * NF * C, TILES * COLS
        xp = sb("xp", [P, XCOLS + 2 * PCOLS])
        X_rows = xp[:, 0:XCOLS].rearrange("p (u s) -> p u s", s=C)
        PX = [xp[:, XCOLS + e * PCOLS:XCOLS + (e + 1) * PCOLS].rearrange("p (t c) -> p t c", t=TILES)
              for e in range(2)]
        T_flat = sb("T_sb", [P, SMP * PF * NF])
        T_sb = T_flat[:, :].rearrange("p (h t z y) -> p h t z y", h=2, t=TILES, z=PF)
        PT = sb("PT", [P, SLOTS, BANK])
        E_q = sb("E_q", [P, FQ, K])
        H_sb = sb("H_sb", [P, BANK])
        H_T = sb("H_T", [P, TILES, C])
        W1c = sb("W1c", [P, PF, C])
        W1h = sb("W1h", [P, PF, C])
        W2c = sb("W2c", [P, PF, P])
        W0z = sb("W0z", [P, NF, C])
        b1_k = sb("b1_k", [P, 2, C])
        W0T = sb("W0T", [P, NCH, C])
        G2_flat = sb("G2_sb", [P, PF * B])
        G2_sb = G2_flat[:, :].rearrange("p (y b) -> p y b", y=PF)
        kept = sb("kept", [P, 2, KEEP])
        ident = sb("ident", [P, P])
        ids_0 = sb("ids_0", [P, NF], INT32)
        ids_g = sb("ids_g", [P, NF], INT32)
        Wt1 = sb("Wt1", [P, 2, 512])
        Wt1d = sb("Wt1d", [DENSE, 512])
        Wt2 = sb("Wt2", [P, 4, 256])
        Wt3 = sb("Wt3", [P, 2])
        dT = sb("dT", [DENSE, B])
        b0_col = sb("b0_col", [P, 1])
        zb = sb("zb", [P, 2])
        zb64 = sb("zb64", [P, 2])
        bt1 = sb("bt1", [P, 4])
        bt2 = sb("bt2", [P, 2])

        raw = XCOLS
        W0_raw = xp[:, raw:raw + 1024].rearrange("p (i z) -> p i z", z=NF)
        W1_raw = xp[:, raw + 1024:raw + 3072].rearrange("p (i z) -> p i z", z=NF)
        W2_raw = xp[:, raw + 3072:raw + 5120].rearrange("p (i z) -> p i z", z=NF)
        W0_sym = xp[0:C, raw + 5120:raw + 5120 + PAIRCOLS]
        d_raw = xp[:, raw + 5888:raw + 5888 + GROUPS * DENSE].rearrange("p (g d) -> p g d", g=GROUPS)
        E_0 = G2_flat[:, 0:NF * K].rearrange("p (z k) -> p z k", z=NF)
        G01 = xp[:, 0:STEPS * KEEP].rearrange("p (n c) -> p n c", n=STEPS)
        G1_all = G01[:, :, 0:G1COLS].rearrange("p n (z s) -> p n z s", z=PF)
        G0_all = G01[:, :, G1COLS:KEEP].rearrange("p n (y c) -> p n y c", y=NF)
        zA = T_flat[:, 0:512]
        zB = T_flat[:, 512:1024]
        h1 = T_flat[:, 1024:3072].rearrange("p (m b) -> p m b", m=4)
        h2 = T_flat[:, 3072:4096].rearrange("p (m b) -> p m b", m=2)
        y_sb = T_flat[0:1, 4096:4608]

        kept_out = nc.dram_tensor("kept_out", [STEPS, P, KEEP], FP32, kind="Internal").ap()

        psT = ps("psT", [P, 4, BANK])
        psP = ps("psP", [P, 2, BANK])
        psH = ps("psH", [P, BANK])
        psG = ps("psG", [P, BANK])

        small_in = sem("small_in")
        w0_in, w1_in, w2_in = sem("w0_in"), sem("w1_in"), sem("w2_in")
        b1_zeroed = sem("b1_zeroed")
        ids0_in, idsg_in = sem("ids0_in"), sem("idsg_in")
        identity = sem("identity")
        w0_sym = sem("w0_sym")
        zb_ready = sem("zb_ready")
        w_tr = sem("w_tr")
        w_evac = sem("w_evac")
        first_rows = [sem(f"first_rows{q}") for q in range(QUARTERS)]
        rows_in = sem("rows_in")
        mirrors_begun = sem("mirrors_begun")
        lookups_begun = sem("lookups_begun")
        x_tr = sem("x_tr")
        x_evac = sem("x_evac")
        px_ready = sem("px_ready")
        px_used = sem("px_used")
        p_tr = sem("p_tr")
        p_evac = sem("p_evac")
        p_used = sem("p_used")
        h_evac = sem("h_evac")
        h_tr = sem("h_tr")
        ht_ready = sem("ht_ready")
        t_ready = sem("t_ready")
        cross_evac = sem("cross_evac")
        own_evac = sem("own_evac")
        mirrored = sem("mirrored")
        g1_kept = sem("g1_kept")
        g0_evac = sem("g0_evac")
        kept_sent = sem("kept_sent")
        kept_free = sem("kept_free")
        turns = sem("turns")
        g2_ready = sem("g2_ready")
        g2_evac = sem("g2_evac")
        g01_in = sem("g01_in")
        z0_ready, z1_ready, z2_ready = sem("z0_ready"), sem("z1_ready"), sem("z2_ready")
        z_evac = sem("z_evac")
        h1_ready, h1_evac = sem("h1_ready"), sem("h1_evac")
        h2_ready, h2_evac = sem("h2_ready"), sem("h2_evac")
        y_ready, y_evac, y_sent = sem("y_ready"), sem("y_evac"), sem("y_sent")

        W_BANKS = 4 + 4 + 4 + 2
        SMALL = 13

        block = ctx.enter_context(nc.Block())

        @block.sync
        def _(sp):
            sp.dma_start(ids_0[:, :], ids[0:P, :]).then_inc(ids0_in, 16)
            sp.dma_start(W1_raw.rearrange("p i z -> p (i z)"), W1).then_inc(w1_in, 16)
            sp.dma_start(W0_raw.rearrange("p i z -> p (i z)"), W0).then_inc(w0_in, 16)
            sp.dma_start(W2_raw.rearrange("p i z -> p (i z)"), W2).then_inc(w2_in, 16)
            sp.dma_start(d_raw, dense_ctx.rearrange("(g p) d -> p g d", p=P)).then_inc(w2_in, 16)
            sp.wait_ge(b1_zeroed, 1)
            for h in range(2):
                sp.dma_start(b1_k[C * h:C * h + C, h, :], b1[0:C].unsqueeze(0).broadcast_to([C, C]))\
                  .then_inc(small_in, 16)
            for lot in range(2):
                sp.dma_start(b0_col[C * lot:C * lot + C, :], b0[0:C].unsqueeze(1)).then_inc(small_in, 16)
            sp.dma_start(zb[0:C, 0:1], b0[C:P].unsqueeze(1)).then_inc(small_in, 16)
            sp.dma_start(zb[C:P, 0:1], b1[C:P].unsqueeze(1)).then_inc(small_in, 16)
            sp.dma_start(zb[:, 1:2], b2.unsqueeze(1)).then_inc(small_in, 16)
            sp.dma_start(Wt1[:, :, :], W_top1[0:2 * P, :].rearrange("(a p) n -> p a n", p=P)).then_inc(small_in, 16)
            sp.dma_start(Wt1d[:, :], W_top1[2 * P:2 * P + DENSE, :]).then_inc(small_in, 16)
            sp.dma_start(Wt2[:, :, :], W_top2.rearrange("(a p) n -> p a n", p=P)).then_inc(small_in, 16)
            sp.dma_start(Wt3[:, :], W_top3.rearrange("(a p) o -> p (a o)", p=P),
                         allow_slow_non_contiguous=True).then_inc(small_in, 16)
            sp.dma_start(bt1[:, :], b_top1.rearrange("(m p) -> p m", p=P),
                         allow_slow_non_contiguous=True).then_inc(small_in, 16)
            sp.dma_start(bt2[:, :], b_top2.rearrange("(m p) -> p m", p=P),
                         allow_slow_non_contiguous=True).then_inc(small_in, 16)

            sp.sem_inc(kept_free, 2)

            def send(n, e):
                sp.wait_ge(g1_kept, n + 1)
                sp.dma_start(kept_out[bass.ds(n, 1), :, :].rearrange("a p c -> (a p) c"), kept[:, e, :])\
                  .then_inc(kept_sent, 16)
                sp.wait_ge(kept_sent, 16 * (n + 1))
                sp.sem_inc(kept_free, 1)

            with sp.Fori(0, PAIRS_OF_STEPS) as r:
                for e in range(2):
                    send(2 * r + e, e)
            sp.wait_ge(px_used, STEPS)
            sp.dma_start(G01, kept_out.rearrange("n p c -> p n c")).then_inc(g01_in, 16)

            sp.wait_ge(y_evac, 1)
            sp.dma_start(y_out.rearrange("b o -> o b"), y_sb).then_inc(y_sent, 16)
            sp.wait_ge(y_sent, 16)

        @block.gpsimd
        def _(pool):
            nc.gpsimd.memset(ident[:, :], 0.0).then_inc(identity, 1)
            pool.wait_ge(identity, 1)
            nc.gpsimd.affine_select(out=ident[:, :], in_=ident[:, :], compare_op=ALU.not_equal, fill=1.0,
                                    base=0, pattern=[[-1, P]], channel_multiplier=1).then_inc(identity, 1)
            pool.wait_ge(ids0_in, 16)
            for z in range(NF):
                nc.gpsimd.indirect_dma_start(
                    out=E_0[:, z, :], out_offset=None, in_=tables[z],
                    in_offset=bass.IndirectOffsetOnAxis(ap=ids_0[:, z:z + 1], axis=0),
                ).then_inc(first_rows[z // FQ], 16)

            def lookups(g, q):
                pool.wait_ge(x_tr, QUARTERS * g + q)
                pool.sem_inc(lookups_begun, 1)
                if q == 0:
                    pool.dma_start(ids_g[:, :], ids[bass.ds(g * P, P), :]).then_inc(idsg_in, 16)
                    pool.wait_ge(idsg_in, 16 * g)
                    pool.sem_inc(lookups_begun, 1)
                for z in range(FQ * q, FQ * q + FQ):
                    nc.gpsimd.indirect_dma_start(
                        out=E_q[:, z - FQ * q, :], out_offset=None, in_=tables[z],
                        in_offset=bass.IndirectOffsetOnAxis(ap=ids_g[:, z:z + 1], axis=0),
                    ).then_inc(rows_in, 16)
                pool.wait_ge(rows_in, 16 * FQ * (QUARTERS * (g - 1) + q + 1))
                pool.sem_inc(lookups_begun, 1)

            def mirror(n):
                pool.wait_ge(own_evac, 2 * TILES * (n + 1))
                pool.sem_inc(mirrors_begun, 1)
                T = T_flat[:, :].rearrange("p (s z y) -> p s z y", s=SMP, z=PF)
                for part in range(2):
                    r = slice(C * part, C * part + C)
                    y0, y1, y2 = PF * part, PF * part + E8, PF * part + PF
                    nc.gpsimd.tensor_copy(T[r, :, E8:PF, y0:y1],
                                          T[r, :, 0:E8, y1:y2].rearrange("p s z y -> p s y z"))\
                        .then_inc(mirrored, 1)
                pool.wait_ge(mirrored, 2 * (n + 1))
                pool.sem_inc(mirrors_begun, 1)

            def pair(g, q, more=True):
                n = 2 * QUARTERS * (g - 1) + 2 * q
                mirror(n)
                if more:
                    lookups(g + (q + 1) // QUARTERS, (q + 1) % QUARTERS)
                mirror(n + 1)

            lookups(1, 0)
            with pool.Fori(1, GROUPS - 1) as g:
                for q in range(QUARTERS):
                    pair(g, q)
            for q in range(QUARTERS):
                pair(GROUPS - 1, q, q < QUARTERS - 1)
            with pool.Fori(2 * LOOKUP_PAIRS, STEPS) as n:
                mirror(n)

        @block.tensor
        def _(pe):
            mm = nc.tensor.matmul

            def transposed_to(out, rows, first, eye):
                n = rows.shape[1]
                return mm(out[first:first + n], rows, eye, start=True, stop=True, tile_position=(0, first))

            def x_transposes(rows, bank):
                for a in range(FQ):
                    for h in range(2):
                        last = transposed_to(psP[:, bank, C * a:C * a + C], rows[:, a, :], C * h,
                                             ident[:, C * h:C * h + C])
                last.then_inc(x_tr, 1)

            def lot_transposes(m, e, c, lot):
                k = 2 * c + lot
                if k >= 2:
                    pe.wait_ge(p_evac, LOTS * m + k - 1)
                c0 = TOP_A + P * c
                for a in range(LOT):
                    last = nc.tensor.transpose(psP[:, lot, P * a:P * a + P],
                                               PX[e][:, lot * LOT + a, c0:c0 + P], ident[:, :])
                last.then_inc(p_tr, 1)

            def h_matmuls(m, e, c):
                k = 2 * c
                pe.wait_ge(p_evac, LOTS * m + k + 2)
                for lot in range(2):
                    last = mm(psH[C * lot:C * lot + C, :], W0T[:, c, :],
                              PT[:, (LOTS * e + k + lot) % SLOTS, :],
                              start=(c == 0), stop=(c == NCH - 1), tile_position=(0, C * lot))
                last.then_inc(p_used, 1)

            def h_transposes(m):
                pe.wait_ge(h_evac, m + 1)
                for a in range(LOT):
                    last = nc.tensor.transpose(psT[:, 0, P * a:P * a + P], H_sb[:, P * a:P * a + P],
                                               ident[:, :])
                last.then_inc(h_tr, 1)

            count = [0]

            def next_bank():
                k = count[0]
                count[0] += 1
                if k >= 4:
                    pe.wait_ge(w_evac, k - 3)
                return psT[:, k % 4, :]

            pe.wait_ge(identity, 2)
            pe.wait_ge(w1_in, 16)
            for z in range(0, PF, 4):
                bank = next_bank()
                for a in range(4):
                    for part in range(2):
                        transposed_to(bank[:, P * a:P * a + C], W1_raw[:, 0:C, PF * part + z + a],
                                      C * part, ident[:, 0:C])
                        last = transposed_to(bank[:, P * a + C:P * a + P],
                                             W1_raw[:, 0:C, PF * (1 - part) + z + a], C * part, ident[:, C:P])
                last.then_inc(w_tr, 1)
            pe.wait_ge(w0_in, 16)
            for y in range(0, NF, 8):
                bank = next_bank()
                for a in range(8):
                    for j in range(4):
                        last = transposed_to(bank[:, C * a:C * a + C], W0_raw[:, :, y + a], NF * j, ident[:, C:P])
                last.then_inc(w_tr, 1)
            pe.wait_ge(w2_in, 32)
            for y in range(0, PF, 4):
                bank = next_bank()
                for a in range(4):
                    for part in range(2):
                        last = transposed_to(bank[:, P * a:P * a + P], W2_raw[:, 0:C, PF * part + y + a],
                                             C * part, ident[:, :])
                last.then_inc(w_tr, 1)
            bank = next_bank()
            for g in range(GROUPS):
                last = nc.tensor.transpose(bank[0:DENSE, P * g:P * g + P], d_raw[:, g, :], ident[:, :])
            last.then_inc(w_tr, 1)
            pe.wait_ge(w0_sym, 1)
            bank = next_bank()
            for c in range(NCH):
                last = nc.tensor.transpose(bank[:, C * c:C * c + C], W0_sym[:, P * c:P * c + P], ident[0:C, 0:C])
            last.then_inc(w_tr, 1)

            for q in range(QUARTERS):
                pe.wait_ge(first_rows[q], 16 * FQ)
                if q >= 2:
                    pe.wait_ge(x_evac, q - 1)
                x_transposes(E_0[:, FQ * q:FQ * q + FQ, :], q % 2)

            pe.wait_ge(w_evac, W_BANKS)
            pe.wait_ge(px_ready, 1)
            for c in range(NCH):
                for lot in range(2):
                    lot_transposes(0, 0, c, lot)
                if c:
                    h_matmuls(0, 0, c - 1)
            h_matmuls(0, 0, NCH - 1)
            h_transposes(0)
            pe.wait_ge(small_in, 16 * SMALL)
            pe.sem_inc(g2_ready, 1)

            def step(n, e, lookups, last_step):
                if lookups:
                    pe.wait_ge(rows_in, 8 * FQ * (n + 2))
                    pe.wait_ge(p_evac, LOTS * (n + 1))
                    x_transposes(E_q, 1)
                pe.wait_ge(ht_ready, 2 * (n + 1))
                pe.wait_ge(g0_evac, n + 1)
                for t in range(TILES):
                    if t >= 2:
                        pe.wait_ge(cross_evac, 2 * (TILES * n + t - 1))
                        pe.wait_ge(own_evac, 2 * (TILES * n + t - 1))
                    if t != 1:
                        pe.sem_inc(turns, 1)
                    for h in range(2):
                        r = slice(C * h, C * h + C)
                        for part, c0 in enumerate((A_FROM, B_FROM)):
                            last = mm(psT[C * part:C * part + C, 2 * (t % 2) + h, 0:TW], H_T[r, t, :],
                                      PX[e][r, t, c0:c0 + TW], start=True, stop=True,
                                      tile_position=(C * h, C * part))
                    last.then_inc(t_ready, 1)

                G = psG[:, 0:SMP * PF].rearrange("p (h t y) -> p h t y", h=2, t=TILES)

                def bias_and_g0():
                    pe.wait_ge(g2_evac, n + 1)
                    pe.sem_inc(turns, 1)
                    for h in range(2):
                        for part in range(2):
                            mm(G[C * part:C * part + C, h], b1_k[:, h, :], PX[e][:, :, PF * part:PF * part + PF],
                               start=(h == 0), stop=False, tile_position=(0, C * part))
                    pe.wait_ge(cross_evac, 2 * TILES * (n + 1))
                    pe.wait_ge(own_evac, 2 * TILES * (n + 1))
                    g2(1)
                    for t in range(TILES):
                        for h in range(2):
                            x = PX[e][C * h:C * h + C, t, 0:NF]
                            j, q = t % 4, t // 4
                            last = mm(psT[NF * j:NF * j + NF, 2 + h, NF * q:NF * q + NF], x, x,
                                      start=True, stop=True, tile_position=(C * h, NF * j))
                    last.then_inc(px_used, 1)

                done = [0]

                def g2(count):
                    for z in range(done[0], min(PF, done[0] + count)):
                        if z == E8:
                            pe.wait_ge(mirrored, 2 * (n + 1))
                            pe.sem_inc(turns, 1)
                        for part in range(2):
                            last = mm(psG[C * part:C * part + C, 0:SMP * PF], W1c[:, z, :],
                                      T_sb[:, :, :, z, PF * part:PF * part + PF].rearrange("p h t y -> p (h t) y"),
                                      start=False, stop=(z == PF - 1), tile_position=(0, C * part))
                        done[0] = z + 1
                        if z == PF - 1:
                            last.then_inc(g2_ready, 1)

                if last_step:
                    bias_and_g0()
                    g2(PF)
                    return
                m, f = n + 1, 1 - e
                pe.wait_ge(px_ready, m + 1)
                if lookups:
                    pe.wait_ge(x_evac, QUARTERS + n // 2 + 1)
                for c in range(NCH):
                    for lot in range(2):
                        lot_transposes(m, f, c, lot)
                    if c == 0:
                        bias_and_g0()
                    else:
                        h_matmuls(m, f, c - 1)
                        g2(2)
                h_matmuls(m, f, NCH - 1)
                g2(2)
                h_transposes(m)
                g2(PF)

            def pair(r, lookups, last_pair=False):
                step(2 * r, 0, lookups, False)
                step(2 * r + 1, 1, False, last_pair)

            with pe.Fori(0, LOOKUP_PAIRS) as r:
                pair(r, True)
            with pe.Fori(LOOKUP_PAIRS, PAIRS_OF_STEPS - 1) as r:
                pair(r, False)
            pair(PAIRS_OF_STEPS - 1, False, True)

            def z0_products(y):
                for j in range(4):
                    r = slice(NF * j, NF * j + NF)
                    last = mm(psT[0:C, j, 0:P].rearrange("p (n c) -> p n c", n=STEPS),
                              W0z[r, y, :], G0_all[r, :, y, :],
                              start=(y == 0), stop=(y == NF - 1), tile_position=(NF * j, 0))
                return last

            pe.wait_ge(g2_evac, STEPS + 1)
            for y in range(PF // 2):
                last2 = mm(psH[:, :], W2c[:, y, :], G2_sb[:, y, :], start=(y == 0), stop=False)
            pe.wait_ge(g01_in, 16)
            for z in range(PF):
                last1 = mm(psP[C:P, 0, :].rearrange("p (n s) -> p n s", n=STEPS), W1h[:, z, :],
                           G1_all[:, :, z, :], start=(z == 0), stop=(z == PF - 1), tile_position=(0, C))
                for y in (2 * z, 2 * z + 1):
                    last0 = z0_products(y)
                if z % 2:
                    y = PF // 2 + z // 2
                    last2 = mm(psH[:, :], W2c[:, y, :], G2_sb[:, y, :], start=False, stop=(y == PF - 1))
            last0.then_inc(z0_ready, 1)
            last1.then_inc(z1_ready, 1)
            last2.then_inc(z2_ready, 1)

            pe.wait_ge(z_evac, 6)
            for m in range(4):
                cols = slice(P * m, P * m + P)
                mm(psT[:, m, :], Wt1[:, 0, cols], zA, start=True, stop=False)
                mm(psT[:, m, :], Wt1[:, 1, cols], zB, start=False, stop=False)
                mm(psT[:, m, :], Wt1d[:, cols], dT[:, :], start=False, stop=True).then_inc(h1_ready, 1)
            for a in range(4):
                pe.wait_ge(h1_evac, a + 1)
                for m in range(2):
                    last = mm(psP[:, m, :], Wt2[:, a, P * m:P * m + P], h1[:, a, :],
                              start=(a == 0), stop=(a == 3))
            last.then_inc(h2_ready, 1)
            pe.wait_ge(h2_evac, 2)
            for a in range(2):
                last = mm(psH[0:1, :], Wt3[:, a:a + 1], h2[:, a, :], start=(a == 0), stop=(a == 1))
            last.then_inc(y_ready, 1)

        @block.scalar
        def _(act):
            copy = nc.scalar.copy

            k = 0

            def weights():
                act.wait_ge(w_tr, k + 1)
                return psT[:, k % 4, :]

            for z in range(0, PF, 4):
                bank = weights().rearrange("p (a o) -> p a o", a=4)
                copy(W1c[:, z:z + 4, :], bank[:, :, 0:C])
                copy(W1h[:, z:z + 4, :], bank[:, :, C:P]).then_inc(w_evac, 1)
                k += 1
            for y in range(0, NF, 8):
                copy(W0z[:, y:y + 8, :], weights().rearrange("p (a o) -> p a o", a=8)).then_inc(w_evac, 1)
                k += 1
            for y in range(0, PF, 4):
                copy(W2c[:, y:y + 4, :], weights().rearrange("p (a o) -> p a o", a=4)).then_inc(w_evac, 1)
                k += 1
            bank = weights()
            for g in range(GROUPS):
                cols = slice(P * g, P * g + P)
                last = copy(dT[:, cols].rearrange("d (n h t) -> d h n t", h=2, t=TILES),
                            bank[0:DENSE, cols].rearrange("d (h n t) -> d h n t", h=2, t=TILES))
            last.then_inc(w_evac, 1)
            k += 1
            copy(W0T[:, :, :], weights()[:, 0:C * NCH].rearrange("p (c i) -> p c i", i=C)).then_inc(w_evac, 1)
            act.wait_ge(small_in, 16 * SMALL)

            def lot_copies(m, e, c):
                for lot in range(2):
                    k = 2 * c + lot
                    act.wait_ge(p_tr, LOTS * m + k + 1)
                    if not (isinstance(m, int) and m == 0 and k < SLOTS):
                        act.wait_ge(p_used, NCH * m + c - 1)
                    copy(PT[:, (LOTS * e + k) % SLOTS, :], psP[:, lot, :]).then_inc(p_evac, 1)

            def next_h(m, e):
                for c in range(NCH):
                    lot_copies(m, e, c)
                act.wait_ge(p_used, NCH * (m + 1))
                nc.scalar.activation(H_sb[:, :], psH[:, :], ACT.Identity, bias=b0_col[:, :])\
                    .then_inc(h_evac, 1)
                act.wait_ge(h_tr, m + 1)
                for lot in range(2):
                    copy(H_T[:, LOT * lot:LOT * lot + LOT, :],
                         psT[:, 0, :].rearrange("p (a l i) -> p a l i", l=2, i=C)[:, :, lot, :])\
                        .then_inc(ht_ready, 1)

            next_h(0, 0)
            act.sem_inc(g2_evac, 1)

            def step(n, e, last_step):
                act.wait_ge(g2_ready, n + 1)
                for t in range(TILES):
                    act.wait_ge(t_ready, TILES * n + t + 1)
                    pair = psT[:, 2 * (t % 2):2 * (t % 2) + 2, :]
                    copy(T_sb[C:P, :, t, :, 0:PF],
                         pair[C:P, :, 0:CROSS].rearrange("p h (y z) -> p h z y", z=PF)).then_inc(cross_evac, 1)
                    act.wait_ge(own_evac, 2 * (TILES * n + t) + 1)
                    copy(T_sb[0:C, :, t, :, PF:NF],
                         pair[0:C, :, TW - CROSS:TW].rearrange("p h (z y) -> p h z y", z=PF))\
                        .then_inc(cross_evac, 1)
                if not last_step:
                    next_h(n + 1, 1 - e)
                act.wait_ge(g2_ready, n + 2)
                copy(G2_sb[:, :, bass.ds(n * SMP, SMP)],
                     psG[:, 0:SMP * PF].rearrange("p (s y) -> p y s", y=PF)).then_inc(g2_evac, 1)

            with act.Fori(0, PAIRS_OF_STEPS - 1) as r:
                for e in range(2):
                    step(2 * r + e, e, False)
            step(STEPS - 2, 0, False)
            step(STEPS - 1, 1, True)

            act.wait_ge(zb_ready, 1)
            act.wait_ge(z0_ready, 1)
            for j in range(4):
                nc.scalar.activation(zA[0:C, j:B:4], psT[0:C, j, 0:P], ACT.Identity,
                                     bias=zb64[0:C, 0:1]).then_inc(z_evac, 1)
            act.wait_ge(z1_ready, 1)
            nc.scalar.activation(zA[C:P, :], psP[C:P, 0, :], ACT.Identity, bias=zb64[C:P, 0:1]).then_inc(z_evac, 1)
            act.wait_ge(z2_ready, 1)
            nc.scalar.activation(zB, psH[:, :], ACT.Identity, bias=zb64[:, 1:2]).then_inc(z_evac, 1)
            for m in range(4):
                act.wait_ge(h1_ready, m + 1)
                nc.scalar.activation(h1[:, m, :], psT[:, m, :], ACT.Relu, bias=bt1[:, m:m + 1])\
                    .then_inc(h1_evac, 1)
            act.wait_ge(h2_ready, 1)
            for m in range(2):
                nc.scalar.activation(h2[:, m, :], psP[:, m, :], ACT.Relu, bias=bt2[:, m:m + 1])\
                    .then_inc(h2_evac, 1)
            act.wait_ge(y_ready, 1)
            for g in range(GROUPS):
                cols = slice(P * g, P * g + P)
                last = copy(y_sb[:, cols].rearrange("o (h n t) -> o h n t", h=2, t=TILES),
                            psH[0:1, cols].rearrange("o (n h t) -> o h n t", h=2, t=TILES))
            last.then_inc(y_evac, 1)

        @block.vector
        def _(dve):
            tt = nc.vector.tensor_tensor
            cp = nc.vector.tensor_copy

            nc.vector.memset(b1_k[:, :, :], 0.0).then_inc(b1_zeroed, 1)
            dve.wait_ge(w0_in, 16)
            w0 = W0_raw[0:C, :, :]
            for part, top, low in ((0, TOP_A, LOW_A), (1, TOP_B, LOW_B)):
                a0, a1, a2 = PF * part, PF * part + E8, PF * part + PF
                t = W0_sym[:, top - TOP_A:top - TOP_A + TOP].rearrange("p (z y) -> p z y", z=E8)
                cp(t[:, :, 0:E8], w0[:, a0:a1, a0:a1])
                tt(t[:, :, E8:PF], w0[:, a0:a1, a1:a2], w0[:, a1:a2, a0:a1].rearrange("p y z -> p z y"), ALU.add)
                cp(W0_sym[:, low - TOP_A:low - TOP_A + LOW].rearrange("p (z y) -> p z y", z=E8),
                   w0[:, a1:a2, a1:a2])
            tt(W0_sym[:, CR - TOP_A:CR - TOP_A + CROSS].rearrange("p (z y) -> p z y", z=PF),
               w0[:, 0:PF, PF:NF], w0[:, PF:NF, 0:PF].rearrange("p y z -> p z y"), ALU.add).then_inc(w0_sym, 1)
            dve.wait_ge(small_in, 16 * SMALL)
            nc.vector.tensor_scalar_mul(zb64[:, :], zb[:, :], float(K)).then_inc(zb_ready, 1)

            def x_copy(bank, out):
                cp(out, psP[:, bank, :].rearrange("p (a s) -> p a s", a=FQ)).then_inc(x_evac, 1)

            def products(e, first_row, first_tile):
                def xt(z, n):
                    return X_rows[:, bass.ds(first_row + z, n), bass.ds(first_tile, TILES)]\
                        .rearrange("p z t -> p t z")

                def outer(col, z, nz, y, ny):
                    tt(PX[e][:, :, col:col + nz * ny].rearrange("p t (z y) -> p t z y", z=nz),
                       xt(z, nz).unsqueeze(3).broadcast_to([P, TILES, nz, ny]),
                       xt(y, ny).unsqueeze(2).broadcast_to([P, TILES, nz, ny]), ALU.mult)

                cp(PX[e][:, :, 0:NF], xt(0, NF))
                cp(PX[e][:, :, X_A2:COLS], xt(0, PF))
                outer(TOP_A, 0, E8, 0, PF)
                outer(LOW_A, E8, E8, E8, E8)
                outer(CR, 0, PF, PF, PF)
                outer(TOP_B, PF, E8, PF, PF)
                z, nz, col = PF + E8, E8, LOW_B
                tt(PX[e][:, :, col:col + LOW].rearrange("p t (z y) -> p t z y", z=nz),
                   xt(z, nz).unsqueeze(3).broadcast_to([P, TILES, nz, nz]),
                   xt(z, nz).unsqueeze(2).broadcast_to([P, TILES, nz, nz]), ALU.mult).then_inc(px_ready, 1)

            for q in range(QUARTERS):
                dve.wait_ge(x_tr, q + 1)
                x_copy(q % 2, X_rows[:, FQ * q:FQ * q + FQ, :])
            dve.wait_ge(x_evac, QUARTERS)
            dve.sem_inc(g0_evac, 1)
            dve.wait_ge(w_tr, W_BANKS)
            products(0, 0, 0)
            products(1, 0, TILES)

            def step(n, e):
                dve.wait_ge(g2_ready, n + 1)
                dve.wait_ge(kept_free, n + 1)
                G1 = kept[:, e, 0:G1COLS].rearrange("p (z h t) -> p h t z", z=PF, h=2)
                for t in range(TILES):
                    dve.wait_ge(t_ready, TILES * n + t + 1)
                    pair = psT[:, 2 * (t % 2):2 * (t % 2) + 2, :]
                    for part, x0, top0 in ((0, 0, PF), (1, TW - PF, CROSS)):
                        if part:
                            dve.wait_ge(cross_evac, 2 * (TILES * n + t) + 1)
                        r = slice(C * part, C * part + C)
                        y0, y1, y2 = PF * part, PF * part + E8, PF * part + PF
                        cp(T_sb[r, :, t, 0:E8, y0:y2],
                           pair[r, :, top0:top0 + TOP].rearrange("p h (z y) -> p h z y", z=E8))
                        cp(T_sb[r, :, t, E8:PF, y1:y2],
                           pair[r, :, top0 + TOP:top0 + TOP + LOW].rearrange("p h (z y) -> p h z y", z=E8))
                        cp(G1[r, :, t, :], pair[r, :, x0:x0 + PF]).then_inc(own_evac, 1)
                dve.wait_ge(px_used, n + 1)
                cp(kept[:, e, G1COLS:KEEP].rearrange("p (y h q) -> p h q y", y=NF, h=2),
                   psT[:, 2:4, 0:2 * NF].rearrange("p h (q y) -> p h q y", y=NF)).then_inc(g0_evac, 1)

            def kept_done(n):
                dve.wait_ge(g0_evac, n + 2)
                dve.sem_inc(g1_kept, 1)

            def pair(r, lookups, more):
                first_row = dve.snap(((r + 1) // QUARTERS) * NF) if more else 0
                first_tile = dve.snap(((r + 1) % QUARTERS) * 2 * TILES) if more else 0
                for e in range(2):
                    if lookups and e == 0:
                        dve.wait_ge(x_tr, QUARTERS + r + 1)
                        x_copy(1, X_rows[:, bass.ds((r + QUARTERS) * FQ, FQ), :])
                    step(2 * r + e, e)
                    if more:
                        if lookups and e == 0:
                            dve.wait_ge(x_evac, QUARTERS + r + 1)
                        products(e, first_row, first_tile + TILES * e)
                    kept_done(2 * r + e)

            with dve.Fori(0, LOOKUP_PAIRS) as r:
                pair(r, True, True)
            with dve.Fori(LOOKUP_PAIRS, PAIRS_OF_STEPS - 1) as r:
                pair(r, False, True)
            pair(PAIRS_OF_STEPS - 1, False, False)


_TABLES = [f"tbl_{f}" for f in range(NF)]
_INS = ["dense_ctx", "ids", *_TABLES, "W_top1", "b_top1", "W_top2", "b_top2", "W_top3",
        "L0_rec_W0", "L0_rec_b0", "L0_rec_W1", "L0_rec_b1", "L0_rec_W2", "L0_rec_b2"]


def kernel(**inputs):
    import numpy as _np
    import concourse.bacc as _bacc
    from concourse import mybir as _mybir
    from concourse.bass_utils import run_bass_kernel_spmd as _run

    nc = _bacc.Bacc("TRN2", target_bir_lowering=False, num_devices=1)
    arrays, aps = {}, {}
    for name in _INS:
        a = _np.ascontiguousarray(inputs[name])
        arrays[f"in_{name}"] = a
        aps[name] = nc.dram_tensor(f"in_{name}", a.shape, _mybir.dt.from_np(a.dtype), kind="ExternalInput").ap()
    y = nc.dram_tensor("y", [B, 1], _mybir.dt.float32, kind="ExternalOutput").ap()
    dlrm_tower(nc, aps["dense_ctx"], aps["ids"], [aps[t] for t in _TABLES],
               aps["W_top1"], aps["b_top1"], aps["W_top2"], aps["b_top2"], aps["W_top3"],
               aps["L0_rec_W0"], aps["L0_rec_b0"], aps["L0_rec_W1"], aps["L0_rec_b1"],
               aps["L0_rec_W2"], aps["L0_rec_b2"], y)
    r = _run(nc, [arrays], core_ids=[0])
    return r.results[0]["y"]
```

```python
from contextlib import ExitStack

import concourse.bass as bass
from concourse import mybir

FP32 = mybir.dt.float32
INT32 = mybir.dt.int32
ALU = mybir.AluOpType
ACT = mybir.ActivationFunctionType

B, NF, K = 512, 32, 64
C = 64
P = 128
DENSE = 16
BANK = 512
GROUPS = B // P
TILES = 8
SMP = 2 * TILES
STEPS = B // SMP
QUARTERS = 4
FQ = NF // QUARTERS
PAIRS_OF_STEPS = STEPS // 2
LOOKUP_PAIRS = PAIRS_OF_STEPS - QUARTERS
PF = NF // 2
E8, E4 = PF // 2, PF // 4
A_BLOCKS = ((0, E4, 0, NF), (E4, E4, E4, NF - E4), (E8, E4, E8, E8), (E8 + E4, E4, E8 + E4, E4))
CROSS_BLOCK = (E8, E8, PF, PF)
B_BLOCKS = tuple((PF + E4 * k, E4, PF + E4 * k, PF - E4 * k) for k in range(4))
BLOCKS = A_BLOCKS + (CROSS_BLOCK,) + B_BLOCKS
ONE, X_ALL = 0, 1
PAIRS = X_ALL + NF


def columns_of(blocks):
    return sum(nz * ny for _, nz, _, ny in blocks)


FIRST = {block: PAIRS + columns_of(BLOCKS[:k]) for k, block in enumerate(BLOCKS)}
PAIRCOLS = columns_of(BLOCKS)
X_A2 = PAIRS + PAIRCOLS
COLS = X_A2 + PF
TW = PF + columns_of(A_BLOCKS)
A_FROM, B_FROM = X_ALL + PF, FIRST[CROSS_BLOCK]
CHUNKS = [(P * c, min(P, PAIRCOLS - P * c)) for c in range(-(-PAIRCOLS // P))]
NCH = len(CHUNKS)
LACKS = ((E4, 0, E4), (E8, 0, E8), (E8 + E4, E8, E4))
LOT = 4
LOTS = 2 * NCH
H_BEFORE = {4: (1,)}
LOTS_AFTER = {0: 0, 2: 1, 3: 2, 4: 3, 6: 4}
H_AFTER = {2: (0,), 5: (2,), 7: (3, 4)}
LOT_0_BY_DVE = (0, 2, 4)
H1_ORDER = (1, 2, 3, 0)
LAST_Y = [block for block in BLOCKS if block[2] + block[3] == NF]
BLOCKS_0_FOR = [sum(FIRST[block] - PAIRS < first + size for block in LAST_Y) for first, size in CHUNKS]
SLOTS = 4
NS = 1 + NF
G1COLS, G0COLS = PF * SMP, NS * SMP // 4
KEEP = G1COLS + G0COLS
ONLY_G0 = G1COLS + SMP // 4
FETCHES, FETCH_DMAS = 3, 1 + 4 * 4
EARLY_GROUPS = GROUPS - 1
EARLY = EARLY_GROUPS * NF * C // KEEP


def dlrm_tower(nc, dense_ctx, ids, tables, W_top1, b_top1, W_top2, b_top2, W_top3,
               W0, b0, W1, b1, W2, b2, y_out):
    ctx = ExitStack()
    with ctx:
        def sb(name, shape, dt=FP32):
            return ctx.enter_context(nc.sbuf_tensor(name, shape, dt))

        def ps(name, shape):
            return ctx.enter_context(nc.psum_tensor(name, shape, FP32))

        def sem(name):
            return ctx.enter_context(nc.semaphore(name))

        XCOLS, PCOLS = GROUPS * NF * C, TILES * COLS
        xp = sb("xp", [P, XCOLS + 2 * PCOLS])
        X_rows = xp[:, 0:XCOLS].rearrange("p (u s) -> p u s", s=C)
        PX = [xp[:, XCOLS + e * PCOLS:XCOLS + (e + 1) * PCOLS].rearrange("p (t c) -> p t c", t=TILES)
              for e in range(2)]
        T_flat = sb("T_sb", [P, SMP * PF * NF])
        T_sb = T_flat[:, :].rearrange("p (h t z y) -> p h t z y", h=2, t=TILES, z=PF)
        PT = sb("PT", [P, SLOTS, BANK])
        E_q = sb("E_q", [P, FQ, K])
        H_sb = sb("H_sb", [P, BANK])
        H_T = sb("H_T", [P, TILES, C])
        W1c = sb("W1c", [P, PF, C])
        W1h = sb("W1h", [P, PF, C])
        W2c = sb("W2c", [P, PF, P])
        W0z = sb("W0z", [P, E8, C])
        V_T = sb("V_T", [P, 4, P])
        b1_all = sb("b1_all", [P, C])
        W0T = sb("W0T", [P, NCH, C])
        G2_flat = sb("G2_sb", [P, PF * B])
        G2_sb = G2_flat[:, :].rearrange("p (y b) -> p y b", y=PF)
        kept = sb("kept", [P, 2, KEEP])
        ident = sb("ident", [P, P])
        ids_0 = sb("ids_0", [P, NF], INT32)
        ids_g = sb("ids_g", [P, NF], INT32)
        Wt1 = sb("Wt1", [P, 2, 512])
        Wt1d = sb("Wt1d", [DENSE, 512])
        Wt2 = sb("Wt2", [P, 4, 256])
        Wt3 = sb("Wt3", [P, 2])
        dT = sb("dT", [DENSE, B])
        b0_col = sb("b0_col", [P, 1])
        zb = sb("zb", [P, 3])
        zb64 = sb("zb64", [P, 3])
        bt1 = sb("bt1", [P, 4])
        bt2 = sb("bt2", [P, 2])

        W0_raw = T_flat[:, 0:1024].rearrange("p (i z) -> p i z", z=NF)
        W1_raw = T_flat[:, 1024:3072].rearrange("p (i z) -> p i z", z=NF)
        W2_raw = T_flat[:, 3072:5120].rearrange("p (i z) -> p i z", z=NF)
        W2_b1 = T_flat[:, 5120:7168].rearrange("p (i z) -> p i z", z=NF)
        W0_sym = T_flat[0:C, 7168:7168 + PAIRCOLS]
        d_raw = T_flat[:, 7808:7808 + GROUPS * DENSE].rearrange("p (g d) -> p g d", g=GROUPS)
        V_raw = T_flat[:, 7936:7936 + NF]
        E_0 = G2_flat[:, 0:NF * K].rearrange("p (z k) -> p z k", z=NF)
        G01 = xp[:, 0:STEPS * KEEP].rearrange("p (n c) -> p n c", n=STEPS)
        G1_all = G01[:, :, 0:G1COLS].rearrange("p n (z s) -> p n z s", z=PF)
        S_all = G01[:, :, G1COLS:ONLY_G0]
        G0_all = G01[:, :, ONLY_G0:KEEP].rearrange("p n (j y c) -> p n j y c", j=4, y=E8)
        zA = T_flat[:, 0:512]
        zB = T_flat[:, 512:1024]
        h1 = T_flat[:, 1024:3072].rearrange("p (m b) -> p m b", m=4)
        h2 = T_flat[:, 3072:4096].rearrange("p (m b) -> p m b", m=2)
        y_sb = T_flat[0:1, 4096:4608]

        kept_out = nc.dram_tensor("kept_out", [STEPS, P, KEEP], FP32, kind="Internal").ap()

        psT = ps("psT", [P, 4, BANK])
        psP = ps("psP", [P, 2, BANK])
        psH = ps("psH", [P, BANK])
        psG = ps("psG", [P, BANK])

        small_in = sem("small_in")
        b1_in = sem("b1_in")
        w0_in, w1_in, w2_in = sem("w0_in"), sem("w1_in"), sem("w2_in")
        zeroed = sem("zeroed")
        v_products, v_raw = sem("v_products"), sem("v_raw")
        ids0_in, idsg_in = sem("ids0_in"), sem("idsg_in")
        identity = sem("identity")
        w0_sym = sem("w0_sym")
        zb_ready = sem("zb_ready")
        w_tr = sem("w_tr")
        w_evac = sem("w_evac")
        first_rows = [sem(f"first_rows{q}") for q in range(QUARTERS)]
        rows_in = sem("rows_in")
        lookups_begun = sem("lookups_begun")
        x_tr = sem("x_tr")
        x_evac = [sem(f"x_evac{k}") for k in range(2)]
        blocks_0 = sem("blocks_0")
        px_ready = sem("px_ready")
        px_used = sem("px_used")
        p_tr = sem("p_tr")
        lot_evac = [sem(f"lot_evac{k}") for k in range(2)]
        p_used = sem("p_used")
        h_evac = sem("h_evac")
        h_tr = sem("h_tr")
        ht_ready = sem("ht_ready")
        t_ready = sem("t_ready")
        a_evac = sem("a_evac")
        b_evac = sem("b_evac")
        filled_in = [sem(f"filled_in{k}") for k in range(3)]
        g1_kept = sem("g1_kept")
        g0_evac = sem("g0_evac")
        kept_sent = sem("kept_sent")
        kept_free = sem("kept_free")
        turns = sem("turns")
        g2_ready = sem("g2_ready")
        g2_evac = sem("g2_evac")
        g01_in = sem("g01_in")
        z0_ready, z1_ready, z2_ready = sem("z0_ready"), sem("z1_ready"), sem("z2_ready")
        za_evac, zb_evac = sem("za_evac"), sem("zb_evac")
        h1_ready, h1_evac = sem("h1_ready"), sem("h1_evac")
        h2_ready, h2_evac = sem("h2_ready"), sem("h2_evac")
        y_ready, y_evac, y_sent = sem("y_ready"), sem("y_evac"), sem("y_sent")

        W_BANKS = 4 + 1 + 4 + 3
        SMALL = 13

        block = ctx.enter_context(nc.Block())

        def x_copy(copy, odd, bank, first_row):
            rows = psP[C * odd:C * odd + C, bank, :].rearrange("p (a h s) -> p h a s", h=2, s=C)
            to = X_rows[:, bass.ds(first_row, FQ), :].rearrange("p (a f) s -> p f a s", f=2)
            for h in range(2):
                last = copy(to[C * h:C * h + C, odd], rows[:, h])
            last.then_inc(x_evac[odd], 1)

        def fill_in(copy, k):
            z, y, count = LACKS[k]
            T = T_flat[:, :].rearrange("p (s z y) -> p s z y", s=SMP, z=PF)
            for part in range(2):
                r, y0 = slice(C * part, C * part + C), PF * part
                copy(T[r, :, z:z + count, y0 + y:y0 + y + count],
                     T[r, :, y:y + count, y0 + z:y0 + z + count].rearrange("p s z y -> p s y z"))\
                    .then_inc(filled_in[k], 1)

        @block.sync
        def _(sp):
            sp.dma_start(ids_0[:, :], ids[0:P, :]).then_inc(ids0_in, 16)
            sp.dma_start(W1_raw.rearrange("p i z -> p (i z)"), W1).then_inc(w1_in, 16)
            sp.dma_start(W0_raw.rearrange("p i z -> p (i z)"), W0).then_inc(w0_in, 16)
            sp.dma_start(W2_raw.rearrange("p i z -> p (i z)"), W2).then_inc(w2_in, 16)
            sp.dma_start(d_raw, dense_ctx.rearrange("(g p) d -> p g d", p=P)).then_inc(w2_in, 16)
            sp.dma_start(b1_all[:, :], b1[0:C].unsqueeze(0).broadcast_to([P, C])).then_inc(b1_in, 16)
            for r in (slice(0, C), slice(C, P)):
                sp.dma_start(b0_col[r, :], b0[0:C].unsqueeze(1)).then_inc(small_in, 16)
                sp.dma_start(zb[r, 0:1], b0[C:P].unsqueeze(1)).then_inc(small_in, 16)
                sp.dma_start(zb[r, 1:2], b1[C:P].unsqueeze(1)).then_inc(small_in, 16)
            sp.dma_start(zb[:, 2:3], b2.unsqueeze(1)).then_inc(small_in, 16)
            sp.dma_start(Wt1[:, :, :], W_top1[0:2 * P, :].rearrange("(a p) n -> p a n", p=P)).then_inc(small_in, 16)
            sp.dma_start(Wt1d[:, :], W_top1[2 * P:2 * P + DENSE, :]).then_inc(small_in, 16)
            sp.dma_start(Wt2[:, :, :], W_top2.rearrange("(a p) n -> p a n", p=P)).then_inc(small_in, 16)
            sp.dma_start(Wt3[:, :], W_top3.rearrange("(a p) o -> p (a o)", p=P),
                         allow_slow_non_contiguous=True).then_inc(small_in, 16)
            sp.dma_start(bt1[:, :], b_top1.rearrange("(m p) -> p m", p=P),
                         allow_slow_non_contiguous=True).then_inc(small_in, 16)
            sp.dma_start(bt2[:, :], b_top2.rearrange("(m p) -> p m", p=P),
                         allow_slow_non_contiguous=True).then_inc(small_in, 16)

            sp.sem_inc(kept_free, 2)

            def send(n, e):
                sp.wait_ge(g1_kept, n + 1)
                sp.dma_start(kept_out[bass.ds(n, 1), :, :].rearrange("a p c -> (a p) c"), kept[:, e, :])\
                  .then_inc(kept_sent, 16)
                sp.wait_ge(kept_sent, 16 * (n + 1))
                sp.sem_inc(kept_free, 1)

            def fetch(n0, n1):
                sp.dma_start(G01[:, n0:n1, 0:ONLY_G0], kept_out[n0:n1, :, 0:ONLY_G0].rearrange("n p c -> p n c"))\
                  .then_inc(g01_in, 16)
                size = (KEEP - ONLY_G0) // 4
                for j in range(4):
                    for y8 in range(4):
                        c = ONLY_G0 + size * y8
                        sp.dma_start(G01[NF * y8:NF * y8 + NF, n0:n1, ONLY_G0 + size * j:ONLY_G0 + size * (j + 1)],
                                     kept_out[n0:n1, NF * j:NF * j + NF, c:c + size].rearrange("n z c -> z n c"))\
                          .then_inc(g01_in, 16)

            early_pairs = EARLY_GROUPS * QUARTERS
            with sp.Fori(0, early_pairs) as r:
                for e in range(2):
                    send(2 * r + e, e)
            sp.wait_ge(px_ready, 2 * early_pairs)
            fetch(0, EARLY)
            with sp.Fori(early_pairs, PAIRS_OF_STEPS - 1) as r:
                for e in range(2):
                    send(2 * r + e, e)
            send(STEPS - 2, 0)
            sp.wait_ge(px_ready, STEPS)
            sp.wait_ge(px_used, STEPS - 1)
            fetch(EARLY, STEPS - 1)
            send(STEPS - 1, 1)
            fetch(STEPS - 1, STEPS)

            sp.wait_ge(y_evac, 1)
            sp.dma_start(y_out.rearrange("b o -> o b"), y_sb).then_inc(y_sent, 16)
            sp.wait_ge(y_sent, 16)

        @block.gpsimd
        def _(pool):
            nc.gpsimd.memset(ident[:, :], 0.0).then_inc(identity, 1)
            pool.wait_ge(identity, 1)
            nc.gpsimd.affine_select(out=ident[:, :], in_=ident[:, :], compare_op=ALU.not_equal, fill=1.0,
                                    base=0, pattern=[[-1, P]], channel_multiplier=1).then_inc(identity, 1)
            pool.wait_ge(ids0_in, 16)
            for z in range(NF):
                nc.gpsimd.indirect_dma_start(
                    out=E_0[:, z, :], out_offset=None, in_=tables[z],
                    in_offset=bass.IndirectOffsetOnAxis(ap=ids_0[:, z:z + 1], axis=0),
                ).then_inc(first_rows[z // FQ], 16)

            def lookups(g, q):
                pool.wait_ge(x_tr, QUARTERS * g + q)
                pool.sem_inc(lookups_begun, 1)
                if q == 0:
                    pool.dma_start(ids_g[:, :], ids[bass.ds(g * P, P), :]).then_inc(idsg_in, 16)
                    pool.wait_ge(idsg_in, 16 * g)
                    pool.sem_inc(lookups_begun, 1)
                for z in range(FQ * q, FQ * q + FQ):
                    nc.gpsimd.indirect_dma_start(
                        out=E_q[:, z - FQ * q, :], out_offset=None, in_=tables[z],
                        in_offset=bass.IndirectOffsetOnAxis(ap=ids_g[:, z:z + 1], axis=0),
                    ).then_inc(rows_in, 16)

            with pool.Fori(1, GROUPS) as g:
                for q in range(QUARTERS):
                    lookups(g, q)

        @block.tensor
        def _(pe):
            mm = nc.tensor.matmul

            def transposed_to(out, rows, first, eye):
                n = rows.shape[1]
                return mm(out[first:first + n], rows, eye, start=True, stop=True, tile_position=(0, first))

            def x_transposes(rows, bank):
                for a in range(FQ // 2):
                    last = nc.tensor.transpose(psP[:, bank, P * a:P * a + P],
                                               rows[:, 2 * a:2 * a + 2, :].rearrange("s f k -> s (f k)"),
                                               ident[:, :])
                last.then_inc(x_tr, 1)

            def lot_transposes(m, e, c, lot):
                if c:
                    pe.wait_ge(lot_evac[lot], NCH * m + c)
                    pe.sem_inc(turns, 1)
                first, size = CHUNKS[c]
                for a in range(LOT):
                    last = nc.tensor.transpose(psP[0:size, lot, P * a:P * a + P],
                                               PX[e][:, lot * LOT + a, PAIRS + first:PAIRS + first + size],
                                               ident[:, :])
                last.then_inc(p_tr, 1)

            def h_matmuls(m, e, c):
                k = 2 * c
                for lot in range(2):
                    pe.wait_ge(lot_evac[lot], NCH * m + c + 1)
                if CHUNKS[c][1] < P:
                    pe.sem_inc(turns, 1)
                r = slice(0, CHUNKS[c][1])
                for lot in range(2):
                    last = mm(psH[C * lot:C * lot + C, :], W0T[r, c, :],
                              PT[r, (LOTS * e + k + lot) % SLOTS, :],
                              start=(c == 0), stop=(c == NCH - 1), tile_position=(0, C * lot))
                last.then_inc(p_used, 1)

            def h_transposes(m):
                pe.wait_ge(h_evac, m + 1)
                for a in range(LOT):
                    last = nc.tensor.transpose(psT[:, 0, P * a:P * a + P], H_sb[:, P * a:P * a + P],
                                               ident[:, :])
                last.then_inc(h_tr, 1)

            count = [0]

            def next_bank():
                k = count[0]
                count[0] += 1
                if k >= 4:
                    pe.wait_ge(w_evac, k - 3)
                return psT[:, k % 4, :]

            def rows_to_xt(q):
                pe.wait_ge(first_rows[q], 16 * FQ)
                if q >= 2:
                    for evac in x_evac:
                        pe.wait_ge(evac, q - 1)
                x_transposes(E_0[:, FQ * q:FQ * q + FQ, :], q % 2)

            def w2_bank(y):
                bank = next_bank()
                for a in range(4):
                    for part in range(2):
                        last = transposed_to(bank[:, P * a:P * a + P], W2_raw[:, 0:C, PF * part + y + a],
                                             C * part, ident[:, :])
                last.then_inc(w_tr, 1)

            pe.wait_ge(identity, 2)
            pe.wait_ge(w1_in, 16)
            for z in range(0, PF, 4):
                bank = next_bank()
                for a in range(4):
                    for part in range(2):
                        transposed_to(bank[:, P * a:P * a + C], W1_raw[:, 0:C, PF * part + z + a],
                                      C * part, ident[:, 0:C])
                        last = transposed_to(bank[:, P * a + C:P * a + P],
                                             W1_raw[:, 0:C, PF * (1 - part) + z + a], C * part, ident[:, C:P])
                last.then_inc(w_tr, 1)
            rows_to_xt(0)
            pe.wait_ge(w0_in, 16)
            bank = next_bank()
            for y in range(E8):
                for y8 in range(4):
                    last = transposed_to(bank[:, C * y:C * y + C], W0_raw[:, :, E8 * y8 + y], NF * y8,
                                         ident[:, C:P])
            last.then_inc(w_tr, 1)
            rows_to_xt(1)
            pe.wait_ge(w0_sym, 1)
            bank = next_bank()
            for c, (first, size) in enumerate(CHUNKS):
                last = nc.tensor.transpose(bank[0:size, C * c:C * c + C], W0_sym[:, first:first + size],
                                           ident[0:C, 0:C])
            last.then_inc(w_tr, 1)
            w0t_bank = count[0]
            pe.wait_ge(v_raw, 1)
            bank = next_bank()
            for j in range(4):
                last = transposed_to(bank[:, 0:P], V_raw, NF * j, ident[:, :])
            last.then_inc(w_tr, 1)
            pe.wait_ge(w2_in, 32)
            bank = next_bank()
            for g in range(GROUPS):
                last = nc.tensor.transpose(bank[0:DENSE, P * g:P * g + P], d_raw[:, g, :], ident[:, :])
            last.then_inc(w_tr, 1)
            for y in (0, 4):
                w2_bank(y)
            rows_to_xt(2)
            for y in (8, 12):
                w2_bank(y)
            rows_to_xt(3)

            pe.wait_ge(w_evac, w0t_bank)
            for c in range(NCH):
                pe.wait_ge(blocks_0, BLOCKS_0_FOR[c])
                for lot in range(2):
                    lot_transposes(0, 0, c, lot)
                if c:
                    h_matmuls(0, 0, c - 1)
            h_matmuls(0, 0, NCH - 1)
            pe.wait_ge(w_evac, W_BANKS)
            h_transposes(0)
            pe.wait_ge(px_ready, 1)
            pe.wait_ge(small_in, 16 * SMALL)
            pe.sem_inc(g2_ready, 1)

            def step(n, e, lookups, last_step):
                m, f = n + 1, 1 - e
                if lookups:
                    pe.wait_ge(rows_in, 8 * FQ * (n + 2))
                    pe.wait_ge(lot_evac[1], NCH * (n + 1))
                    x_transposes(E_q, 1)
                if last_step:
                    pe.wait_ge(g2_evac, STEPS // 2 + 1)
                pe.wait_ge(ht_ready, 2 * (n + 1))
                pe.wait_ge(g0_evac, n + 1)
                for t in range(TILES):
                    if t >= 2:
                        pe.wait_ge(a_evac, TILES * n + t - 1)
                        pe.wait_ge(b_evac, TILES * n + t - 1)
                    if t != 1:
                        pe.sem_inc(turns, 1)
                    for h in range(2):
                        r = slice(C * h, C * h + C)
                        for part, c0 in enumerate((A_FROM, B_FROM)):
                            last = mm(psT[C * part:C * part + C, 2 * (t % 2) + h, 0:TW], H_T[r, t, :],
                                      PX[e][r, t, c0:c0 + TW], start=True, stop=True,
                                      tile_position=(C * h, C * part))
                    last.then_inc(t_ready, 1)
                    if last_step:
                        for y in (2 * t, 2 * t + 1):
                            mm(psH[:, 0:B // 2], W2c[:, y, :], G2_sb[:, y, 0:B // 2], start=(y == 0), stop=False)
                        continue
                    for c in H_BEFORE.get(t, ()):
                        h_matmuls(m, f, c)
                    if t in LOTS_AFTER:
                        if t == 0:
                            pe.wait_ge(px_ready, m + 1)
                            if lookups:
                                for evac in x_evac:
                                    pe.wait_ge(evac, QUARTERS + n // 2 + 1)
                        for lot in range(2):
                            lot_transposes(m, f, LOTS_AFTER[t], lot)
                    for c in H_AFTER.get(t, ()):
                        h_matmuls(m, f, c)

                def g0():
                    pe.wait_ge(g2_evac, n + 1)
                    pe.wait_ge(a_evac, TILES * (n + 1))
                    pe.wait_ge(b_evac, TILES * (n + 1))
                    g2(1)
                    for t in range(TILES):
                        for h in range(2):
                            x = PX[e][C * h:C * h + C, t, ONE:ONE + NS]
                            j, q = t % 4, t // 4
                            last = mm(psT[NF * j:NF * j + NF, 2 + h, NS * q:NS * q + NS], x[:, 1:], x,
                                      start=True, stop=True, tile_position=(C * h, NF * j))
                    last.then_inc(px_used, 1)

                done = [0]

                def g2(count):
                    for z in range(done[0], min(PF, done[0] + count)):
                        for k, lack in enumerate(LACKS):
                            if z == lack[0]:
                                pe.wait_ge(filled_in[k], 2 * (n + 1))
                        for part in range(2):
                            last = mm(psG[C * part:C * part + C, 0:SMP * PF], W1c[:, z, :],
                                      T_sb[:, :, :, z, PF * part:PF * part + PF].rearrange("p h t y -> p (h t) y"),
                                      start=(z == 0), stop=(z == PF - 1), tile_position=(0, C * part))
                        done[0] = z + 1
                        if z == PF - 1:
                            last.then_inc(g2_ready, 1)

                g0()
                if not last_step:
                    g2(2)
                    h_transposes(m)
                g2(PF)

            def pair(r, lookups, last_pair=False):
                step(2 * r, 0, lookups, False)
                step(2 * r + 1, 1, False, last_pair)

            with pe.Fori(0, LOOKUP_PAIRS) as r:
                pair(r, True)
            with pe.Fori(LOOKUP_PAIRS, PAIRS_OF_STEPS - 1) as r:
                pair(r, False)
            pair(PAIRS_OF_STEPS - 1, False, True)

            pe.wait_ge(g2_evac, STEPS + 1)
            for y in range(PF):
                mm(psP[:, 1, 0:B // 2], W2c[:, y, :], G2_sb[:, y, B // 2:B], start=(y == 0), stop=False)
            pe.wait_ge(g01_in, 16 * FETCHES * FETCH_DMAS)
            for half, bank in enumerate((psH[:, :], psP[:, 1, :])):
                n0 = STEPS // 2 * half
                for j in range(4):
                    last = mm(bank[:, j:B // 2:4].rearrange("p (n c) -> p n c", n=STEPS // 2), V_T[:, j, :],
                              S_all[:, n0:n0 + STEPS // 2, :], start=False, stop=(j == 3))
            last.then_inc(z2_ready, 1)
            for z in range(PF):
                for half in range(2):
                    n0 = STEPS // 2 * half
                    last = mm(psP[C * half:C * half + C, 0, 0:B // 2].rearrange("p (n s) -> p n s", s=SMP),
                              W1h[:, z, :], G1_all[:, n0:n0 + STEPS // 2, z, :],
                              start=(z == 0), stop=(z == PF - 1), tile_position=(0, C * half))
            last.then_inc(z1_ready, 1)
            for y in range(E8):
                for half in range(2):
                    n0 = STEPS // 2 * half
                    last = mm(psT[C * half:C * half + C, 0, 0:B // 2]
                              .rearrange("p (n j c) -> p n j c", n=STEPS // 2, j=4),
                              W0z[:, y, :], G0_all[:, n0:n0 + STEPS // 2, :, y, :],
                              start=(y == 0), stop=(y == E8 - 1), tile_position=(0, C * half))
            last.then_inc(z0_ready, 1)

            def h1_parts(m, first):
                cols = slice(P * m, P * m + P)
                if first:
                    mm(psT[:, m, :], Wt1[:, 1, cols], zB, start=True, stop=False)
                    mm(psT[:, m, :], Wt1d[:, cols], dT[:, :], start=False, stop=False)
                else:
                    mm(psT[:, m, :], Wt1[:, 0, cols], zA, start=False, stop=True).then_inc(h1_ready, 1)

            pe.wait_ge(zb_evac, 2)
            for m in H1_ORDER[:3]:
                h1_parts(m, True)
            pe.wait_ge(za_evac, 4)
            for m in H1_ORDER[:3]:
                h1_parts(m, False)
            h1_parts(0, True)
            h1_parts(0, False)
            for k, a in enumerate(H1_ORDER):
                pe.wait_ge(h1_evac, k + 1)
                for m in range(2):
                    last = mm(psP[:, m, :], Wt2[:, a, P * m:P * m + P], h1[:, a, :],
                              start=(k == 0), stop=(k == 3))
                    if k == 3:
                        last.then_inc(h2_ready, 1)
            for a in range(2):
                pe.wait_ge(h2_evac, a + 1)
                last = mm(psH[0:1, :], Wt3[:, a:a + 1], h2[:, a, :], start=(a == 0), stop=(a == 1))
            last.then_inc(y_ready, 1)

        @block.scalar
        def _(act):
            copy = nc.scalar.copy

            k = 0

            def weights():
                act.wait_ge(w_tr, k + 1)
                return psT[:, k % 4, :]

            def rows_copy(q):
                act.wait_ge(x_tr, q + 1)
                x_copy(copy, 1, q % 2, FQ * q)

            for z in range(0, PF, 4):
                bank = weights().rearrange("p (a o) -> p a o", a=4)
                copy(W1c[:, z:z + 4, :], bank[:, :, 0:C])
                copy(W1h[:, z:z + 4, :], bank[:, :, C:P]).then_inc(w_evac, 1)
                k += 1
            rows_copy(0)
            copy(W0z[:, :, :], weights().rearrange("p (y o) -> p y o", y=E8)).then_inc(w_evac, 1)
            k += 1
            rows_copy(1)
            bank = weights()
            for c, (first, size) in enumerate(CHUNKS):
                last = copy(W0T[0:size, c, :], bank[0:size, C * c:C * c + C])
            last.then_inc(w_evac, 1)
            k += 1
            act.wait_ge(zeroed, 1)
            bank = weights()
            for j in range(4):
                r = slice(NF * j, NF * j + NF)
                last = copy(V_T[r, j, :], bank[r, 0:P])
            last.then_inc(w_evac, 1)
            k += 1
            bank = weights()
            for g in range(GROUPS):
                cols = slice(P * g, P * g + P)
                last = copy(dT[:, cols].rearrange("d (n h t) -> d h n t", h=2, t=TILES),
                            bank[0:DENSE, cols].rearrange("d (h n t) -> d h n t", h=2, t=TILES))
            last.then_inc(w_evac, 1)
            k += 1
            for q, ys in ((2, (0, 4)), (3, (8, 12))):
                for y in ys:
                    copy(W2c[:, y:y + 4, :], weights().rearrange("p (a o) -> p a o", a=4)).then_inc(w_evac, 1)
                    k += 1
                rows_copy(q)
            act.wait_ge(small_in, 16 * SMALL)

            def lot_copy(m, e, c, lot):
                act.wait_ge(p_tr, LOTS * m + 2 * c + lot + 1)
                if not (isinstance(m, int) and m == 0 and c < 2):
                    act.wait_ge(p_used, NCH * m + c - 1)
                r = slice(0, CHUNKS[c][1])
                copy(PT[r, (LOTS * e + 2 * c + lot) % SLOTS, :], psP[r, lot, :]).then_inc(lot_evac[lot], 1)

            def h_copy(m):
                act.wait_ge(p_used, NCH * (m + 1))
                nc.scalar.activation(H_sb[:, :], psH[:, :], ACT.Identity, bias=b0_col[:, :])\
                    .then_inc(h_evac, 1)

            def h_t_copies(m):
                act.wait_ge(h_tr, m + 1)
                for lot in range(2):
                    copy(H_T[:, LOT * lot:LOT * lot + LOT, :],
                         psT[:, 0, :].rearrange("p (a l i) -> p a l i", l=2, i=C)[:, :, lot, :])\
                        .then_inc(ht_ready, 1)

            for c in range(NCH):
                for lot in range(2):
                    lot_copy(0, 0, c, lot)
            h_copy(0)
            h_t_copies(0)
            act.sem_inc(g2_evac, 1)

            def step(n, e, last_step):
                act.wait_ge(g2_ready, n + 1)
                act.wait_ge(kept_free, n + 1)
                G1 = kept[:, e, 0:G1COLS].rearrange("p (z h t) -> p h t z", z=PF, h=2)
                own, other = slice(C, P), slice(0, C)
                for t in range(TILES):
                    act.wait_ge(t_ready, TILES * n + t + 1)
                    pair = psT[own, 2 * (t % 2):2 * (t % 2) + 2, :]
                    for block in (CROSS_BLOCK,) + B_BLOCKS:
                        z, nz, y, ny = block
                        first = FIRST[block] - B_FROM
                        here = pair[:, :, first:first + nz * ny].rearrange("p h (z y) -> p h z y", z=nz)
                        if z < PF:
                            copy(T_sb[other, :, t, z:z + nz, y:y + ny], here)
                            copy(T_sb[own, :, t, :, z:z + nz], here.rearrange("p h z y -> p h y z"))
                        else:
                            copy(T_sb[own, :, t, z - PF:z - PF + nz, y:y + ny], here)
                    copy(G1[own, :, t, :], pair[:, :, TW - PF:TW]).then_inc(b_evac, 1)
                    if not last_step and t in LOTS_AFTER:
                        c = LOTS_AFTER[t]
                        for lot in range(c in LOT_0_BY_DVE, 2):
                            lot_copy(n + 1, 1 - e, c, lot)
                if not last_step:
                    h_copy(n + 1)
                act.wait_ge(a_evac, TILES * (n + 1))
                act.wait_ge(b_evac, TILES * (n + 1))
                fill_in(copy, 1)
                if not last_step:
                    h_t_copies(n + 1)
                act.wait_ge(g2_ready, n + 2)
                copy(G2_sb[:, :, bass.ds(n * SMP, SMP)],
                     psG[:, 0:SMP * PF].rearrange("p (s y) -> p y s", y=PF)).then_inc(g2_evac, 1)

            with act.Fori(0, LOOKUP_PAIRS) as r:
                act.wait_ge(x_tr, QUARTERS + r + 1)
                x_copy(copy, 1, 1, (r + QUARTERS) * FQ)
                for e in range(2):
                    step(2 * r + e, e, False)
            with act.Fori(LOOKUP_PAIRS, PAIRS_OF_STEPS - 1) as r:
                for e in range(2):
                    step(2 * r + e, e, False)
            step(STEPS - 2, 0, False)
            step(STEPS - 1, 1, True)

            act.wait_ge(zb_ready, 1)
            act.wait_ge(z2_ready, 1)
            for half, bank in enumerate((psH[:, :], psP[:, 1, :])):
                nc.scalar.activation(zB[:, B // 2 * half:B // 2 * (half + 1)], bank[:, 0:B // 2], ACT.Identity,
                                     bias=zb64[:, 2:3]).then_inc(zb_evac, 1)
            act.wait_ge(z1_ready, 1)
            for half in range(2):
                r = slice(C * half, C * half + C)
                cols = slice(B // 2 * half, B // 2 * half + B // 2)
                nc.scalar.activation(zA[C:P, cols], psP[r, 0, 0:B // 2], ACT.Identity,
                                     bias=zb64[r, 1:2]).then_inc(za_evac, 1)
            act.wait_ge(z0_ready, 1)
            for half in range(2):
                r = slice(C * half, C * half + C)
                cols = slice(B // 2 * half, B // 2 * half + B // 2)
                nc.scalar.activation(zA[0:C, cols].rearrange("p (n c j) -> p n j c", n=STEPS // 2, j=4),
                                     psT[r, 0, 0:B // 2].rearrange("p (n j c) -> p n j c", n=STEPS // 2, j=4),
                                     ACT.Identity, bias=zb64[r, 0:1]).then_inc(za_evac, 1)
            for k, m in enumerate(H1_ORDER):
                act.wait_ge(h1_ready, k + 1)
                nc.scalar.activation(h1[:, m, :], psT[:, m, :], ACT.Relu, bias=bt1[:, m:m + 1])\
                    .then_inc(h1_evac, 1)
            for m in range(2):
                act.wait_ge(h2_ready, m + 1)
                nc.scalar.activation(h2[:, m, :], psP[:, m, :], ACT.Relu, bias=bt2[:, m:m + 1])\
                    .then_inc(h2_evac, 1)
            act.wait_ge(y_ready, 1)
            for g in range(GROUPS):
                cols = slice(P * g, P * g + P)
                last = copy(y_sb[:, cols].rearrange("o (h n t) -> o h n t", h=2, t=TILES),
                            psH[0:1, cols].rearrange("o (n h t) -> o h n t", h=2, t=TILES))
            last.then_inc(y_evac, 1)

        @block.vector
        def _(dve):
            tt = nc.vector.tensor_tensor
            cp = nc.vector.tensor_copy

            nc.vector.memset(V_T[:, :, :], 0.0).then_inc(zeroed, 1)
            dve.wait_ge(w0_in, 16)
            w0 = W0_raw[0:C, :, :]
            for block in BLOCKS:
                z, nz, y, ny = block
                first = FIRST[block] - PAIRS
                out = W0_sym[:, first:first + nz * ny].rearrange("p (z y) -> p z y", z=nz)
                both = nz if y == z else 0
                if both:
                    last = cp(out[:, :, 0:both], w0[:, z:z + nz, y:y + both])
                if both < ny:
                    last = tt(out[:, :, both:ny], w0[:, z:z + nz, y + both:y + ny],
                              w0[:, y + both:y + ny, z:z + nz].rearrange("p y z -> p z y"), ALU.add)
            last.then_inc(w0_sym, 1)

            dve.wait_ge(w2_in, 32)
            dve.wait_ge(b1_in, 16)
            tt(W2_b1, W2_raw, b1_all[:, :].unsqueeze(2).broadcast_to([P, C, NF]), ALU.mult).then_inc(v_products, 1)
            dve.wait_ge(v_products, 1)
            nc.vector.tensor_reduce(V_raw, W2_b1.rearrange("p i z -> p z i"), mybir.AxisListType.X, ALU.add)\
                .then_inc(v_raw, 1)
            dve.wait_ge(small_in, 16 * SMALL)
            nc.vector.tensor_scalar_mul(zb64[:, :], zb[:, :], float(K)).then_inc(zb_ready, 1)

            def xt(first_row, first_tile, z, n):
                return X_rows[:, bass.ds(first_row + z, n), bass.ds(first_tile, TILES)]\
                    .rearrange("p z t -> p t z")

            def outer(e, first_row, first_tile, block, y0, ny):
                z, nz, y, width = block
                first = FIRST[block]
                return tt(PX[e][:, :, first:first + nz * width]
                          .rearrange("p t (z y) -> p t z y", z=nz)[:, :, :, y0 - y:y0 - y + ny],
                          xt(first_row, first_tile, z, nz).unsqueeze(3).broadcast_to([P, TILES, nz, ny]),
                          xt(first_row, first_tile, y0, ny).unsqueeze(2).broadcast_to([P, TILES, nz, ny]),
                          ALU.mult)

            def x_of(e, first_row, first_tile):
                cp(PX[e][:, :, X_ALL:X_ALL + NF], xt(first_row, first_tile, 0, NF))
                return cp(PX[e][:, :, X_A2:COLS], xt(first_row, first_tile, 0, PF))

            def products(e, first_row, first_tile):
                for block in BLOCKS:
                    outer(e, first_row, first_tile, block, block[2], block[3])
                x_of(e, first_row, first_tile).then_inc(px_ready, 1)

            for e in range(2):
                nc.vector.memset(PX[e][:, :, ONE:ONE + 1], 1.0)
            for q in range(QUARTERS):
                dve.wait_ge(x_tr, q + 1)
                x_copy(cp, 0, q % 2, FQ * q)
                for evac in x_evac:
                    dve.wait_ge(evac, q + 1)
                for block in BLOCKS:
                    y0, y1 = max(block[2], FQ * q), min(block[2] + block[3], FQ * q + FQ)
                    if y0 < y1:
                        last = outer(0, 0, 0, block, y0, y1 - y0)
                        if q == QUARTERS - 1:
                            last.then_inc(blocks_0, 1)
            x_of(0, 0, 0).then_inc(px_ready, 1)
            dve.sem_inc(g0_evac, 1)
            products(1, 0, TILES)

            def lot_copy(m, e, c):
                dve.wait_ge(p_tr, LOTS * m + 2 * c + 1)
                dve.wait_ge(p_used, NCH * m + c - 1)
                r = slice(0, CHUNKS[c][1])
                cp(PT[r, (LOTS * e + 2 * c) % SLOTS, :], psP[r, 0, :]).then_inc(lot_evac[0], 1)

            def step(n, e, last_step):
                dve.wait_ge(g2_ready, n + 1)
                dve.wait_ge(kept_free, n + 1)
                G1 = kept[:, e, 0:G1COLS].rearrange("p (z h t) -> p h t z", z=PF, h=2)
                own, other = slice(0, C), slice(C, P)
                for t in range(TILES):
                    dve.wait_ge(t_ready, TILES * n + t + 1)
                    pair = psT[own, 2 * (t % 2):2 * (t % 2) + 2, :]
                    for block in A_BLOCKS:
                        z, nz, y, ny = block
                        first = FIRST[block] - A_FROM
                        here = pair[:, :, first:first + nz * ny].rearrange("p h (z y) -> p h z y", z=nz)
                        cp(T_sb[own, :, t, z:z + nz, y:y + ny], here)
                        if y + ny > PF:
                            cp(T_sb[other, :, t, :, z:z + nz],
                               here[:, :, :, PF - y:ny].rearrange("p h z y -> p h y z"))
                    cp(G1[own, :, t, :], pair[:, :, 0:PF]).then_inc(a_evac, 1)
                    if not last_step and LOTS_AFTER.get(t) in LOT_0_BY_DVE:
                        lot_copy(n + 1, 1 - e, LOTS_AFTER[t])
                dve.wait_ge(a_evac, TILES * (n + 1))
                dve.wait_ge(b_evac, TILES * (n + 1))
                fill_in(cp, 0)
                fill_in(cp, 2)
                dve.wait_ge(px_used, n + 1)
                cp(kept[:, e, G1COLS:KEEP].rearrange("p (y h q) -> p h q y", y=NS, h=2),
                   psT[:, 2:4, 0:2 * NS].rearrange("p h (q y) -> p h q y", y=NS)).then_inc(g0_evac, 1)

            def kept_done(n):
                dve.wait_ge(g0_evac, n + 2)
                dve.sem_inc(g1_kept, 1)

            def pair(r, lookups, more):
                first_row = dve.snap(((r + 1) // QUARTERS) * NF) if more else 0
                first_tile = dve.snap(((r + 1) % QUARTERS) * 2 * TILES) if more else 0
                for e in range(2):
                    if lookups and e == 0:
                        dve.wait_ge(x_tr, QUARTERS + r + 1)
                        x_copy(cp, 0, 1, (r + QUARTERS) * FQ)
                    step(2 * r + e, e, e == 1 and not more)
                    if more:
                        if lookups and e == 0:
                            for evac in x_evac:
                                dve.wait_ge(evac, QUARTERS + r + 1)
                        products(e, first_row, first_tile + TILES * e)
                    kept_done(2 * r + e)

            with dve.Fori(0, LOOKUP_PAIRS) as r:
                pair(r, True, True)
            with dve.Fori(LOOKUP_PAIRS, PAIRS_OF_STEPS - 1) as r:
                pair(r, False, True)
            pair(PAIRS_OF_STEPS - 1, False, False)


_TABLES = [f"tbl_{f}" for f in range(NF)]
_INS = ["dense_ctx", "ids", *_TABLES, "W_top1", "b_top1", "W_top2", "b_top2", "W_top3",
        "L0_rec_W0", "L0_rec_b0", "L0_rec_W1", "L0_rec_b1", "L0_rec_W2", "L0_rec_b2"]


def kernel(**inputs):
    import numpy as _np
    import concourse.bacc as _bacc
    from concourse import mybir as _mybir
    from concourse.bass_utils import run_bass_kernel_spmd as _run

    nc = _bacc.Bacc("TRN2", target_bir_lowering=False, num_devices=1)
    arrays, aps = {}, {}
    for name in _INS:
        a = _np.ascontiguousarray(inputs[name])
        arrays[f"in_{name}"] = a
        aps[name] = nc.dram_tensor(f"in_{name}", a.shape, _mybir.dt.from_np(a.dtype), kind="ExternalInput").ap()
    y = nc.dram_tensor("y", [B, 1], _mybir.dt.float32, kind="ExternalOutput").ap()
    dlrm_tower(nc, aps["dense_ctx"], aps["ids"], [aps[t] for t in _TABLES],
               aps["W_top1"], aps["b_top1"], aps["W_top2"], aps["b_top2"], aps["W_top3"],
               aps["L0_rec_W0"], aps["L0_rec_b0"], aps["L0_rec_W1"], aps["L0_rec_b1"],
               aps["L0_rec_W2"], aps["L0_rec_b2"], y)
    r = _run(nc, [arrays], core_ids=[0])
    return r.results[0]["y"]
```
